# Optimizing a Trainium2 kernel written in Bass

```python
import numpy as np
import jax
import jax.numpy as jnp

def _softmax(x, axis=-1):
    return jax.nn.softmax(x, axis=axis)

def _gelu(x):
    return jax.nn.gelu(x, approximate=True)

def _silu(x):
    return jax.nn.silu(x)

def _sigmoid(x):
    return jax.nn.sigmoid(x)

def _layernorm(x, axis=-1, eps=1e-05):
    m = jnp.mean(x, axis=axis, keepdims=True)
    v = jnp.var(x, axis=axis, keepdims=True)
    return (x - m) / jnp.sqrt(v + eps)

def _scatter_add(tgt, idx, src, axis=0):
    return tgt.at[idx].add(src)

def _segment_sum(src, seg, n):
    return jax.ops.segment_sum(src, seg, n)
kernel_name = 'mk_prb_d1_jaxref_r4_eef77a'

def setup_inputs(seed: int=0):
    np.random.seed(seed)
    _w = jnp.asarray

    def _L0_attn_setup():
        import jax, jax.numpy as jnp
        import numpy as np
        B, T, D, H = (2, 512, 256, 16)
        DH = D // H
        ROPE_BASE = 10000.0

        def _rope(Xh, cos, sin):
            x0 = Xh[..., 0::2]
            x1 = Xh[..., 1::2]
            r0 = cos * x0 - sin * x1
            r1 = sin * x0 + cos * x1
            return jnp.stack((r0, r1), axis=-1).reshape(Xh.shape)
        key = jax.random.key(seed)
        ks = jax.random.split(key, 5)
        s = 1.0 / np.sqrt(D)
        return {'X': jax.random.normal(ks[0], (B, T, D), dtype=jnp.float32), 'W_q': jax.random.normal(ks[1], (D, D), dtype=jnp.float32) * s, 'W_k': jax.random.normal(ks[2], (D, D), dtype=jnp.float32) * s, 'W_v': jax.random.normal(ks[3], (D, D), dtype=jnp.float32) * s, 'W_o': jax.random.normal(ks[4], (D, D), dtype=jnp.float32) * s}
    _L0_attn_in = _L0_attn_setup()

    def _L0_ffn_setup():
        import jax, jax.numpy as jnp
        import numpy as np
        FP8_E4M3_MAX = 448.0

        def fake_quant_fp8(t):
            amax = jnp.max(jnp.abs(t))
            scale = FP8_E4M3_MAX / jnp.maximum(amax, 1e-12)
            q = (t * scale).astype(jnp.float8_e4m3fn).astype(jnp.float32)
            return q / scale
        key = jax.random.key(seed)
        k1, k2, k3 = jax.random.split(key, 3)
        d_in, d_out = (256, 256)
        x = jax.random.normal(k1, (4, 2048, d_in), dtype=jnp.float32)
        weight = jax.random.normal(k2, (d_out, d_in), dtype=jnp.float32) * (1.0 / np.sqrt(d_in))
        bias = jax.random.normal(k3, (d_out,), dtype=jnp.float32) * 0.01
        return {'x': x, 'weight': weight, 'bias': bias}
    _L0_ffn_in = _L0_ffn_setup()
    _d = {'L0_attn_X': _L0_attn_in['X'], 'L0_attn_W_q': _L0_attn_in['W_q'], 'L0_attn_W_k': _L0_attn_in['W_k'], 'L0_attn_W_v': _L0_attn_in['W_v'], 'L0_attn_W_o': _L0_attn_in['W_o'], 'L0_ffn_weight': _L0_ffn_in['weight'], 'L0_ffn_bias': _L0_ffn_in['bias']}
    _x0 = _d['L0_attn_X']
    _d['L0_attn_X'] = jax.random.normal(jax.random.fold_in(jax.random.key(seed), 1), (8, 512, 256), dtype=_x0.dtype)
    del _x0
    return _d

def reference(L0_attn_X, L0_attn_W_q, L0_attn_W_k, L0_attn_W_v, L0_attn_W_o, L0_ffn_weight, L0_ffn_bias):

    def _L0_attn_ref(X, W_q, W_k, W_v, W_o):
        import jax, jax.numpy as jnp
        import numpy as np
        B, T, D, H = (2, 512, 256, 16)
        DH = D // H
        ROPE_BASE = 10000.0

        def _rope(Xh, cos, sin):
            x0 = Xh[..., 0::2]
            x1 = Xh[..., 1::2]
            r0 = cos * x0 - sin * x1
            r1 = sin * x0 + cos * x1
            return jnp.stack((r0, r1), axis=-1).reshape(Xh.shape)
        b, t, d = X.shape
        Q = X @ W_q.T
        K = X @ W_k.T
        V = X @ W_v.T
        Qh = Q.reshape(b, t, H, DH).transpose(0, 2, 1, 3)
        Kh = K.reshape(b, t, H, DH).transpose(0, 2, 1, 3)
        Vh = V.reshape(b, t, H, DH).transpose(0, 2, 1, 3)
        theta = ROPE_BASE ** (-2.0 * jnp.arange(DH // 2, dtype=jnp.float32) / DH)
        pos = jnp.arange(t, dtype=jnp.float32)
        angles = pos[:, None] * theta[None, :]
        cos = jnp.cos(angles).astype(Qh.dtype)
        sin = jnp.sin(angles).astype(Qh.dtype)
        Qr = _rope(Qh, cos, sin)
        Kr = _rope(Kh, cos, sin)
        scores = jnp.einsum('bhqd,bhkd->bhqk', Qr, Kr) * DH ** (-0.5)
        causal = jnp.triu(jnp.ones((t, t), dtype=bool), 1)
        neg = jnp.finfo(scores.dtype).min
        scores = jnp.where(causal[None, None], neg, scores)
        pattern = jax.nn.softmax(scores, axis=-1)
        heads = jnp.einsum('bhqk,bhkd->bhqd', pattern, Vh)
        out = heads.transpose(0, 2, 1, 3).reshape(b, t, d)
        return out @ W_o.T

    def _L0_ffn_ref(x, weight, bias):
        import jax, jax.numpy as jnp
        import numpy as np
        FP8_E4M3_MAX = 448.0

        def fake_quant_fp8(t):
            amax = jnp.max(jnp.abs(t))
            scale = FP8_E4M3_MAX / jnp.maximum(amax, 1e-12)
            q = (t * scale).astype(jnp.float8_e4m3fn).astype(jnp.float32)
            return q / scale
        xq = fake_quant_fp8(x)
        wq = fake_quant_fp8(weight)
        return jnp.einsum('bsd,od->bso', xq, wq) + bias
    x = L0_attn_X
    xn = _layernorm(x, axis=-1)
    x = x + _L0_attn_ref(xn, L0_attn_W_q, L0_attn_W_k, L0_attn_W_v, L0_attn_W_o) + _L0_ffn_ref(xn, L0_ffn_weight, L0_ffn_bias)
    return x

_drawn_inputs = setup_inputs


def setup_inputs(seed=0):
    import zlib

    import numpy as np

    out = dict(_drawn_inputs(seed))
    spreads = {}
    factors = {'L0_ffn_bias': 8.0}
    for name, (base, spread) in spreads.items():
        noise = np.random.default_rng([zlib.crc32(name.encode()), seed]).standard_normal(out[name].shape)
        drawn = base * np.exp(spread * noise) if base else spread * noise
        out[name] = jnp.asarray(drawn.astype(out[name].dtype))
    for name, factor in factors.items():
        out[name] = (out[name] * factor).astype(out[name].dtype)
    return out
```

```python
from contextlib import ExitStack

import numpy as np

import concourse.bass as bass
from concourse import mybir

F32 = mybir.dt.float32
BF16 = mybir.dt.bfloat16
U32 = mybir.dt.uint32
ALU = mybir.AluOpType
ACT = mybir.ActivationFunctionType
AX = mybir.AxisListType

P = 128
NB, T, D = 8, 512, 256
H, DH = 16, 16
J = DH // 2
NQ = T // P
NC = D // P
HG = 4
NG = H // HG
SLOTS = 5 * NG
PAIR = 2 * T
SCALE = float(DH) ** -0.5
EPS = 1e-5
FP8_MAX = 448.0
NEG = -3.0e38
Q_PARTS = (0, 0, 0, 1, 1, 2)
K_PARTS = (0, 1, 2, 0, 1, 0)
ROWS = 6 * DH
SHIFT = 2

MISC = [(0, "qk", 0), (0, "qk", 1), (1, "v", 0), (2, "v", 1), (3, "o", 0), (4, "o", 1),
        (5, "o", 2), (6, "o", 3), (7, "qk", 2), (8, "qk", 3), (9, "at", 0), (10, "mt", 0),
        (11, "fin", 0), (12, "at", 1), (13, "fin", 1), (14, "at", 2), (15, "fin", 2),
        (16, "at", 3), (17, "fin", 3), (19, "mt", 1)]
ITEMS = [3, 3, 3, 3, 4, 3, 3, 3, 3, 4, 4, 4, 4, 4, 4, 3, 3, 3, 3, 0]
FIRST_ITEM = [sum(ITEMS[:s]) for s in range(SLOTS)]
assert sum(ITEMS) == H * NQ and sum(ITEMS[:10]) == H * NQ // 2


def wait_past(eng, sem, count):
    if not (isinstance(count, int) and count <= 0):
        eng.wait_ge(sem, count)


def over_pairs(eng, body):
    body(0)
    with eng.Fori(1, NB // 2) as i:
        body(i)


def unit_parts(u):
    if u < 2:
        return [(2 * u + i, 0, T * i) for i in range(2)]
    if u < 4:
        return [(2 * (u - 2) + i, kb, T * i + (P if kb == 1 else 0)) for i in range(2) for kb in (3, 1)]
    return [(i, 2, 2 * P * i) for i in range(4)]


def attention_ffn_block(nc, x, wq, wk, wv, wo, wf, bias, cos, sin, out):
    with ExitStack() as ctx:
        def sb(name, shape, dt=F32):
            return ctx.enter_context(nc.sbuf_tensor(name, shape, dt))

        def pb(name, shape):
            return ctx.enter_context(nc.psum_tensor(name, shape, F32))

        def sem(name):
            return ctx.enter_context(nc.semaphore(name))

        wq_sb = sb("wq_sb", [P, NC, 2, P])
        wk_sb = sb("wk_sb", [P, NC, 2, P])
        wv_sb = sb("wv_sb", [P, NC, D])
        wo_sb = sb("wo_sb", [P, NC, D])
        wf_sb = sb("wf_sb", [P, NC, D])
        wf_q = sb("wf_q", [P, NC, D], BF16)
        bias_sb = sb("bias_sb", [P, D])
        cos_sb = sb("cos_sb", [P, T])
        sin_sb = sb("sin_sb", [P, T])
        ident = sb("ident", [P, P])
        ones2 = sb("ones2", [2, P])
        causal = sb("causal", [P, T])
        xnT = sb("xnT", [P, NC, NB * T])
        xn_v = sb("xn_v", [P, NC, T])
        q_st = sb("q_st", [P, 2, H, T], BF16)
        k_st = sb("k_st", [P, 2, H, T], BF16)
        v_sb = sb("v_sb", [P, NQ, H, 2 * DH])
        prob = [sb(f"prob{u}", [P, PAIR]) for u in range(5)]
        heads = sb("heads", [P, NG, T])
        prod = sb("prod", [P, 4, T])
        rot = sb("rot", [P, 2, T])
        rem = sb("rem", [P, 2, T])
        parts = sb("parts", [P, 2, 3, 2, T], BF16)
        scratch = sb("scratch", [P, 2, T], BF16)
        rowmax = sb("rowmax", [P, H * NQ])
        shift = sb("shift", [H * NQ // 2, SHIFT, P], BF16)
        rden = sb("rden", [P, H])
        attn = sb("attn", [P, NQ, D])
        attnT = sb("attnT", [P, 2, NC, P])
        x_res = sb("x_res", [P, NQ, D])
        xq = sb("xq", [P, NC, T], BF16)
        stats = sb("stats", [P, 2, NQ, 6])
        mv_b = sb("mv_b", [P, 2, NQ, 2])
        mv = sb("mv", [P, NB * NQ, 2])
        ve = sb("ve", [P, NB * NQ])
        half = sb("half", [P, NB * NQ])
        rstd = sb("rstd", [P, NB * NQ])
        amax = sb("amax", [P, NB + 1])
        amax2 = sb("amax2", [P, 2])
        amax_r = sb("amax_r", [2, 1])
        amax_d = sb("amax_d", [2, 2])
        amax_b = sb("amax_b", [P, 2])
        inv = sb("inv", [P, 2])
        scale = sb("scale", [P, 2])
        unscale = sb("unscale", [P, 2])
        both = sb("both", [P, 1])
        x_all = q_st[:, :, :, :].rearrange("p a h t -> p (a h t)").bitcast(F32).rearrange(
            "p (b n d) -> p b n d", b=NB, n=NQ)
        xn = [prob[i][:, :].rearrange("p (n d) -> p n d", n=NQ) for i in range(2)]
        qv = sb("qv", [P, NC * T])
        qe = sb("qe", [P, NC * T])

        st_ps = [pb(f"st_ps{i}", [P, PAIR]) for i in range(2)]
        s_ps = [pb(f"s_ps{i}", [P, T]) for i in range(2)]
        o_ps = pb("o_ps", [P, T])
        m_ps = pb("m_ps", [P, T])

        qk_dram = nc.dram_tensor("qk_parts", [2, 2, 3, 2, J, H, T], BF16, kind="Internal").ap()
        shift_dram = nc.dram_tensor("shift_rows", [2, SHIFT, H * NQ // 2, P], BF16, kind="Internal").ap()

        w_in = sem("w_in")
        x_in = [sem(f"x_in{i}") for i in range(2)]
        xnv_in = sem("xnv_in")
        res_in = sem("res_in")
        parts_out = sem("parts_out")
        stack_in = [sem(f"stack_in{g}") for g in range(NG)]
        shift_out = [sem(f"shift_out{i}") for i in range(2)]
        shift_in = [sem(f"shift_in{i}") for i in range(2)]
        y_out = sem("y_out")
        consts = sem("consts")
        ln_stat = sem("ln_stat")
        ln_agg = sem("ln_agg")
        ln_mv = sem("ln_mv")
        ln_ve = sem("ln_ve")
        ln_rstd = sem("ln_rstd")
        xn_done = sem("xn_done")
        xn_turned = sem("xn_turned")
        xnT_copied = sem("xnT_copied")
        amax_done = sem("amax_done")
        amax_turned = sem("amax_turned")
        wquant = sem("wquant")
        st_full = sem("st_full")
        s_full = sem("s_full")
        full = {k: sem(f"{k}_full") for k in ("qk", "v", "o", "at", "fin", "mt")}
        pv_done = sem("pv_done")
        exp_done = sem("exp_done")
        max_done = sem("max_done")
        roped = sem("roped")
        v_copied = sem("v_copied")
        heads_copied = sem("heads_copied")
        recip_done = sem("recip_done")
        normed = sem("normed")
        at_copied = sem("at_copied")
        ffn_added = sem("ffn_added")
        fin_done = sem("fin_done")
        shift_hi = sem("shift_hi")
        shift_done = sem("shift_done")
        masked = sem("masked")
        max_begun = sem("max_begun")
        mask_begun = sem("mask_begun")
        agg_begun = sem("agg_begun")
        rotated = sem("rotated")
        hi_done = sem("hi_done")
        rem_done = sem("rem_done")
        mid_done = sem("mid_done")
        low_done = sem("low_done")
        qv_done = sem("qv_done")
        qe_done = sem("qe_done")
        qc_done = sem("qc_done")
        qw_done = sem("qw_done")
        xq_done = sem("xq_done")
        res_done = sem("res_done")

        reader = {"qk": (roped, 4), "v": (v_copied, 2), "o": (normed, 4), "at": (at_copied, 4),
                  "fin": (fin_done, 4), "mt": (shift_done, 2)}
        ahead = {"qk": 2, "v": 0, "o": -1, "at": -1, "fin": -1, "mt": 1}

        def work(stages):
            need = {"qk": 1, "mt": 2, "v": 3, "o": 4, "at": 4, "fin": 4}
            return [m for m in MISC if need[m[1]] in stages]

        block = ctx.enter_context(nc.Block())

        LOOP = (2, 6)

        def run(eng, iteration):
            iteration(-2, 0, {1})
            iteration(-1, 1, {1, 2})
            iteration(0, 0, {1, 2, 3})
            iteration(1, 1, {1, 2, 3, 4})
            with eng.Fori(0, (LOOP[1] - LOOP[0]) // 2) as i:
                iteration(2 * i + LOOP[0], 0, {1, 2, 3, 4})
                iteration(2 * i + LOOP[0] + 1, 1, {1, 2, 3, 4})
            iteration(6, 0, {2, 3, 4})
            iteration(7, 1, {3, 4})
            iteration(8, 0, {4})

        @block.sync
        def _(eng):
            for dst, src in ((wq_sb, wq), (wk_sb, wk)):
                eng.dma_start(dst[:, :, :, :], src.rearrange("(c p) r m -> p c r m", p=P)).then_inc(w_in, 16)
            for dst, src in ((wv_sb, wv), (wo_sb, wo), (wf_sb, wf)):
                eng.dma_start(dst[:, :, :], src.rearrange("(c p) n -> p c n", p=P)).then_inc(w_in, 16)
            eng.dma_start(cos_sb[:, :], cos).then_inc(w_in, 16)
            eng.dma_start(sin_sb[:, :], sin).then_inc(w_in, 16)
            eng.dma_start(bias_sb[:, :], bias.partition_broadcast(P)).then_inc(w_in, 16)
            def load_x(i):
                for p in range(2):
                    wait_past(eng, x_in[p], 16 * i)
                    eng.dma_start(x_all[:, bass.ds(2 * i + p, 1)].rearrange("p a n d -> p (a n) d"),
                                  x[bass.ds(2 * i + p, 1)].rearrange("a (n p) d -> p (a n) d", p=P))\
                       .then_inc(x_in[p], 16)

            over_pairs(eng, load_x)
            eng.wait_ge(xnT_copied, 2 * NB)
            eng.dma_start(xn_v[:, :, :], xnT[:, :, 0:T]).then_inc(xnv_in, 16)

            def iteration(b, par, stages):
                if 4 in stages:
                    wait_past(eng, y_out, 16 * (b - 1))
                    eng.dma_start(x_res[:, :, :], x[bass.ds(b - 1, 1)].rearrange("a (n p) d -> p (a n) d", p=P))\
                       .then_inc(res_in, 16)
                if 3 in stages and 2 in stages:
                    eng.wait_ge(full["v"], 2 * (b + 1))
                    eng.dma_start(xn_v[:, :, :], xnT[:, :, bass.ds((b + 1) * T, T)]).then_inc(xnv_in, 16)
                if 1 in stages:
                    n = b + 2
                    eng.wait_ge(low_done, 2 * n + 1)
                    eng.dma_start(qk_view(par, 0),
                                  parts[:, 0].rearrange("p t r n -> p (t r) n")).then_inc(parts_out, 16)
                if 2 in stages:
                    shift_rows(b, par, 0)
                if 1 in stages:
                    eng.wait_ge(low_done, 2 * n + 2)
                    eng.dma_start(qk_view(par, 1),
                                  parts[:, 1].rearrange("p t r n -> p (t r) n")).then_inc(parts_out, 16)
                    eng.wait_ge(parts_out, 32 * (n + 1))
                    for g in range(NG - 1):
                        read_stack(b, par, g, 3 in stages)
                if 4 in stages:
                    eng.wait_ge(fin_done, 4 * b)
                    eng.dma_start(out[bass.ds(b - 1, 1)].rearrange("a (n p) d -> p (a n) d", p=P),
                                  x_res[:, :, :]).then_inc(y_out, 16)
                if 1 in stages:
                    read_stack(b, par, NG - 1, 3 in stages)
                if 2 in stages:
                    shift_rows(b, par, 1)

            def qk_view(par, which):
                return qk_dram[par, which].rearrange("t r j h n -> (j h) (t r) n")

            def read_stack(b, par, g, busy):
                if busy:
                    eng.wait_ge(st_full, SLOTS * b + 5 * (g + 1))
                h0 = g * HG
                for which, dst, terms in ((0, q_st, [(t, Q_PARTS[t], 1) for t in range(6)]),
                                          (1, k_st, [(0, 0, 3), (3, 0, 2), (5, 0, 1)])):
                    src = qk_dram[par, which].rearrange("t r j h n -> (t r j) h n")
                    for t, part, n in terms:
                        eng.dma_start(dst[DH * t:DH * (t + n), par, h0:h0 + HG, :],
                                      src[DH * part:DH * (part + n), h0:h0 + HG, :]).then_inc(stack_in[g], 16)

            def shift_rows(b, par, half_):
                eng.wait_ge(shift_done, 2 * (b + 1) + half_ + 1)
                eng.dma_start(shift_dram[half_].rearrange("t a n -> a t n"), shift[:, :, :])\
                   .then_inc(shift_out[half_], 16)
                eng.wait_ge(shift_out[half_], 16 * (b + 2))
                h0 = half_ * (H // 2)
                eng.dma_start(q_st[ROWS:ROWS + SHIFT, 1 - par, h0:h0 + H // 2, :],
                              shift_dram[half_].rearrange("t a n -> t (a n)").rearrange(
                                  "t (h n) -> t h n", h=H // 2)).then_inc(shift_in[half_], 16)

            run(eng, iteration)
            eng.wait_ge(y_out, 16 * NB)

        @block.gpsimd
        def _(eng):
            eng.memset(ident[:, :], 0.0).then_inc(consts, 1)
            eng.memset(causal[:, :], 0.0).then_inc(consts, 1)
            eng.memset(ones2[:, :], 1.0).then_inc(consts, 1)
            eng.memset(half[:, :], -0.5).then_inc(consts, 1)
            eng.memset(v_sb[:, :, :, :], 1.0).then_inc(consts, 1)
            eng.wait_ge(consts, 5)
            eng.memset(k_st[ROWS:ROWS + SHIFT, :, :, :].rearrange("p a h t -> p (a h t)").bitcast(F32),
                       float(np.array([0x3F803F80], np.uint32).view(np.float32)[0])).then_inc(consts, 1)
            eng.wait_ge(consts, 6)
            eng.affine_select(out=ident[:, :], in_=ident[:, :], compare_op=ALU.not_equal, fill=1.0,
                              base=0, pattern=[[-1, P]], channel_multiplier=1).then_inc(consts, 1)
            eng.affine_select(out=causal[:, T - P:T], in_=causal[:, T - P:T], compare_op=ALU.is_ge, fill=NEG,
                              base=0, pattern=[[-1, P]], channel_multiplier=1).then_inc(consts, 1)
            eng.wait_ge(ln_ve, 1)
            eng.tensor_tensor(rstd[:, :], ve[:, :], half[:, :], ALU.pow).then_inc(ln_rstd, 1)

            def iteration(b, par, stages):
                n = b + 2

                def mask(s):
                    u = s % 5
                    if u < 2:
                        ap, pat = prob[u].rearrange("p (h q) -> p h q", h=2)[:, :, 0:P], [[0, 2], [1, P]]
                    elif u < 4:
                        ap = prob[u].rearrange("p (h q) -> p h q", h=2)[:, :, 0:2 * P]
                        pat = [[0, 2], [0, 2], [1, P]]
                    else:
                        ap, pat = prob[u].rearrange("p (h q) -> p h q", h=4)[:, :, 0:P], [[0, 4], [1, P]]
                    eng.wait_ge(exp_done, SLOTS * b + s + 1)
                    eng.sem_inc(mask_begun)
                    eng.affine_select(out=ap, in_=ap, compare_op=ALU.is_ge, fill=0.0, base=0,
                                      pattern=pat, channel_multiplier=-1).then_inc(masked, 1)

                def rotate(w):
                    eng.wait_ge(roped, 4 * n + 2 * w + 2)
                    wait_past(eng, low_done, 2 * n + w)
                    eng.tensor_tensor(rot[:, 0, :], prod[:, 0, :], prod[:, 2, :], ALU.subtract).then_inc(rotated, 1)
                    eng.tensor_tensor(rot[:, 1, :], prod[:, 1, :], prod[:, 3, :], ALU.add).then_inc(rotated, 1)

                def remainder(w):
                    eng.wait_ge(rotated, 4 * n + 2 * w + 2)
                    eng.wait_ge(hi_done, 2 * n + w + 1)
                    eng.tensor_tensor(rem[:, :, :], rot[:, :, :], parts[:, w, 0], ALU.subtract).then_inc(rem_done, 1)

                def low(w):
                    eng.wait_ge(mid_done, 2 * n + w + 1)
                    eng.tensor_tensor(parts[:, w, 2], rem[:, :, :], parts[:, w, 1], ALU.subtract).then_inc(low_done, 1)

                for s in range(SLOTS):
                    if 3 in stages:
                        mask(s)
                    if 1 in stages:
                        if s in (1, 9):
                            rotate(s // 9)
                        if s in (4, 11):
                            remainder(s // 11)
                        if s in (6, 13):
                            low(s // 13)
                    if 4 in stages:
                        if s == 2:
                            eng.wait_ge(res_in, 16 * b)
                            eng.tensor_tensor(x_res[:, :, :], x_res[:, :, :],
                                              bias_sb[:, None, :].to_broadcast([P, NQ, D]), ALU.add)\
                               .then_inc(res_done, 1)
                        if s == 5:
                            eng.wait_ge(qc_done, b)
                            eng.tensor_tensor(qv[:, :], qv[:, :], qe[:, :], ALU.add).then_inc(qw_done, 1)
                        if s == 7:
                            eng.wait_ge(qw_done, b)
                            wait_past(eng, full["fin"], 4 * (b - 1))
                            eng.tensor_tensor(xq.rearrange("p c t -> p (c t)"), qv[:, :], qe[:, :],
                                              ALU.subtract).then_inc(xq_done, 1)

            eng.wait_ge(w_in, 16 * 8)
            run(eng, iteration)

        @block.vector
        def _(eng):
            with eng.Fori(0, NB // 2) as i:
                for p in range(2):
                    eng.wait_ge(x_in[p], 16 * (i + 1))
                    for t in range(NQ):
                        eng.bn_stats(stats[:, p, t, :],
                                     x_all[:, bass.ds(2 * i + p, 1), t, :].rearrange("p a d -> p (a d)"))\
                           .then_inc(ln_stat, 1)
                    eng.wait_ge(ln_stat, 8 * i + 4 * (p + 1))
                    eng.sem_inc(agg_begun)
                    for t in range(NQ):
                        eng.bn_aggr(mv_b[:, p, t, :], stats[:, p, t, :]).then_inc(ln_agg, 1)
                    eng.wait_ge(ln_agg, 8 * i + 4 * (p + 1))
                    eng.tensor_copy(mv[:, bass.ds((2 * i + p) * NQ, NQ), :], mv_b[:, p, :, :]).then_inc(ln_mv, 1)
            eng.wait_ge(ln_mv, NB)
            eng.tensor_scalar(ve[:, :], mv[:, :, 1], EPS, None, ALU.add).then_inc(ln_ve, 1)
            eng.wait_ge(ln_rstd, 1)
            def normalise(i):
                for p in range(2):
                    if p == 0:
                        wait_past(eng, xn_turned, 4 * i - 2)
                    else:
                        wait_past(eng, xn_turned, 4 * i)
                    for t in range(NQ):
                        row = (2 * i + p) * NQ + t
                        eng.tensor_scalar(xn[p][:, t, :],
                                          x_all[:, bass.ds(2 * i + p, 1), t, :].rearrange("p a d -> p (a d)"),
                                          mv[:, bass.ds(row, 1), 0], rstd[:, bass.ds(row, 1)],
                                          ALU.subtract, ALU.mult).then_inc(xn_done, 1)
                    eng.wait_ge(xn_done, 8 * i + 4 * (p + 1))
                    eng.tensor_reduce(amax[:, bass.ds(2 * i + p, 1)], xn[p], AX.XY, ALU.max,
                                      apply_absolute_value=True).then_inc(amax_done, 1)

            over_pairs(eng, normalise)
            eng.wait_ge(w_in, 16 * 8)
            eng.tensor_reduce(amax[:, NB:NB + 1], wf_sb[:, :, :], AX.XY, ALU.max,
                              apply_absolute_value=True).then_inc(amax_done, 1)
            eng.wait_ge(amax_done, NB + 1)
            eng.tensor_reduce(amax2[:, 0:1], amax[:, 0:NB], AX.X, ALU.max).then_inc(amax_done, 1)
            eng.tensor_copy(amax2[:, 1:2], amax[:, NB:NB + 1]).then_inc(amax_done, 1)
            eng.wait_ge(amax_turned, 1)
            eng.tensor_reduce(amax_r[:, :], m_ps[0:2, 0:P], AX.X, ALU.max).then_inc(wquant, 1)
            eng.wait_ge(consts, 8)
            eng.wait_ge(wquant, 1)
            eng.tensor_scalar(amax_d[:, :], ident[0:2, 0:2], amax_r[:, 0:1], None, ALU.mult).then_inc(wquant, 1)
            eng.wait_ge(amax_turned, 2)
            eng.tensor_scalar(amax_b[:, :], m_ps[:, 0:2], 1e-12, None, ALU.max).then_inc(wquant, 1)
            eng.wait_ge(wquant, 3)
            eng.reciprocal(inv[:, :], amax_b[:, :]).then_inc(wquant, 1)
            eng.tensor_scalar(unscale[:, :], amax_b[:, :], 1.0 / FP8_MAX, None, ALU.mult).then_inc(wquant, 1)
            eng.wait_ge(wquant, 5)
            eng.tensor_scalar(scale[:, :], inv[:, :], FP8_MAX, None, ALU.mult).then_inc(wquant, 1)
            eng.tensor_tensor(both[:, :], unscale[:, 0:1], unscale[:, 1:2], ALU.mult).then_inc(wquant, 1)
            eng.wait_ge(wquant, 7)
            nw = NC * D
            wf_f = wf_sb[:, :, :].rearrange("p c n -> p (c n)")
            eng.tensor_scalar(qv[:, 0:nw], wf_f, scale[:, 1:2], None, ALU.mult).then_inc(wquant, 1)
            eng.wait_ge(wquant, 8)
            eng.tensor_scalar(qe[:, 0:nw].bitcast(U32), qv[:, 0:nw].bitcast(U32), 0x7F800000, None,
                              ALU.bitwise_and).then_inc(wquant, 1)
            eng.wait_ge(wquant, 9)
            eng.tensor_scalar(qe[:, 0:nw], qe[:, 0:nw], 2.0 ** -6, 1.5 * 2.0 ** 20, ALU.max, ALU.mult)\
               .then_inc(wquant, 1)
            eng.wait_ge(wquant, 10)
            eng.tensor_tensor(qv[:, 0:nw], qv[:, 0:nw], qe[:, 0:nw], ALU.add).then_inc(wquant, 1)
            eng.wait_ge(wquant, 11)
            eng.tensor_tensor(wf_q[:, :, :].rearrange("p c n -> p (c n)"), qv[:, 0:nw], qe[:, 0:nw],
                              ALU.subtract).then_inc(wquant, 1)
            eng.wait_ge(wquant, 12)

            def iteration(b, par, stages):
                def row_max(e):
                    qb = e % NQ
                    eng.wait_ge(s_full, H * NQ * (b + 1) + e + 1)
                    if e == 0:
                        wait_past(eng, full["mt"], 2 * (b + 1))
                    eng.sem_inc(max_begun)
                    w = P * (qb + 1)
                    eng.tensor_tensor_reduce(scratch[:, e % 2, 0:w], s_ps[e % 2][:, 0:w], causal[:, T - w:T],
                                             1.0, NEG, ALU.add, ALU.max, rowmax[:, e:e + 1])\
                       .then_inc(max_done, 1)

                def rope(k):
                    n = b + 2
                    r = k % 2
                    eng.wait_ge(full["qk"], 4 * n + k + 1)
                    if r == 0:
                        wait_past(eng, rotated, 4 * n + k)
                    a, c = (prod[:, 0, :], prod[:, 1, :]) if r == 0 else (prod[:, 3, :], prod[:, 2, :])
                    eng.tensor_tensor(a, m_ps[:, :], cos_sb[:, :], ALU.mult)
                    eng.tensor_tensor(c, m_ps[:, :], sin_sb[:, :], ALU.mult).then_inc(roped, 1)

                def norm(qb):
                    o = m_ps[:, :].rearrange("p (h w) -> p h w", h=H)
                    eng.wait_ge(full["o"], 4 * (b - 1) + qb + 1)
                    wait_past(eng, normed, 4 * (b - 1) + qb)
                    eng.reciprocal(rden[:, :, None], o[:, :, DH:DH + 1]).then_inc(recip_done, 1)
                    eng.wait_ge(recip_done, 4 * (b - 1) + qb + 1)
                    if qb == 0:
                        wait_past(eng, full["at"], 4 * (b - 1))
                    eng.tensor_tensor(attn[:, qb, :].rearrange("p (h w) -> p h w", h=H), o[:, :, 0:DH],
                                      rden[:, :, None].to_broadcast([P, H, DH]), ALU.mult).then_inc(normed, 1)

                def finish(qb):
                    eng.wait_ge(full["fin"], 4 * (b - 1) + qb + 1)
                    if qb == 0:
                        eng.wait_ge(res_done, b)
                    eng.scalar_tensor_tensor(out=x_res[:, qb, :], in0=m_ps[:, D:2 * D], scalar=both[:, 0:1],
                                             in1=x_res[:, qb, :], op0=ALU.mult, op1=ALU.add)\
                       .then_inc(ffn_added, 1)
                    eng.wait_ge(ffn_added, 4 * (b - 1) + qb + 1)
                    eng.tensor_tensor(x_res[:, qb, :], m_ps[:, 0:D], x_res[:, qb, :], ALU.add)\
                       .then_inc(fin_done, 1)

                def split_max(i):
                    c = 2 * (b + 1) + i
                    rows = H * NQ // 2
                    eng.wait_ge(full["mt"], c + 1)
                    if i == 1:
                        eng.wait_ge(shift_out[0], 16 * (b + 2))
                    else:
                        wait_past(eng, shift_out[1], 16 * (b + 1))
                    eng.tensor_scalar(shift[:, 0, :], m_ps[0:rows, 0:P], -1.0, None, ALU.mult).then_inc(shift_hi, 1)
                    eng.wait_ge(shift_hi, c + 1)
                    eng.scalar_tensor_tensor(out=shift[:, 1, :], in0=m_ps[0:rows, 0:P], scalar=-1.0,
                                             in1=shift[:, 0, :], op0=ALU.mult, op1=ALU.subtract)\
                       .then_inc(shift_done, 1)

                for s in range(SLOTS):
                    if 2 in stages:
                        for e in range(FIRST_ITEM[s], FIRST_ITEM[s] + ITEMS[s]):
                            row_max(e)
                    for slot, kind, k in work(stages):
                        if slot == s and kind in ("qk", "o", "fin", "mt"):
                            {"qk": rope, "o": norm, "fin": finish, "mt": split_max}[kind](k)
                    if s == 3 and 4 in stages:
                        wait_past(eng, xq_done, b - 1)
                        eng.tensor_scalar(qv[:, :].rearrange("p (c t) -> p c t", c=NC),
                                          xnT[:, :, bass.ds((b - 1) * T, T)],
                                          scale[:, 0:1], None, ALU.mult).then_inc(qv_done, 1)
                        eng.wait_ge(qv_done, b)
                        eng.tensor_scalar(qe[:, :].bitcast(U32), qv[:, :].bitcast(U32), 0x7F800000, None,
                                          ALU.bitwise_and).then_inc(qe_done, 1)
                        eng.wait_ge(qe_done, b)
                        eng.tensor_scalar(qe[:, :], qe[:, :], 2.0 ** -6, 1.5 * 2.0 ** 20, ALU.max, ALU.mult)\
                           .then_inc(qc_done, 1)

            run(eng, iteration)

        @block.scalar
        def _(eng):
            with eng.Fori(0, NB // 2) as i:
                for p in range(2):
                    for c in range(NC):
                        eng.wait_ge(xn_turned, 4 * i + 2 * p + c + 1)
                        eng.copy(xnT[:, c, bass.ds((2 * i + p) * T, T)], st_ps[p][:, c * T:(c + 1) * T])\
                           .then_inc(xnT_copied, 1)
            eng.wait_ge(consts, 8)

            def iteration(b, par, stages):
                n = b + 2

                def high(w):
                    eng.wait_ge(rotated, 4 * n + 2 * w + 2)
                    wait_past(eng, parts_out, 32 * n)
                    eng.copy(parts[:, w, 0], rot[:, :, :]).then_inc(hi_done, 1)

                def middle(w):
                    eng.wait_ge(rem_done, 2 * n + w + 1)
                    eng.copy(parts[:, w, 1], rem[:, :, :]).then_inc(mid_done, 1)

                def exp(s):
                    u = s % 5
                    eng.wait_ge(st_full, SLOTS * b + s + 1)
                    g = s // 5
                    if (g > 0 or not isinstance(b, int) or b > 0):
                        eng.wait_ge(pv_done, 12 * b + 3 * (g - 1) + (1, 1, 2, 2, 3)[u])
                    eng.activation(prob[u][:, :], st_ps[s % 2][:, :], ACT.Exp, scale=SCALE).then_inc(exp_done, 1)

                def copy_v(i):
                    eng.wait_ge(full["v"], 2 * b + i + 1)
                    if i == 0:
                        wait_past(eng, pv_done, 12 * b)
                    eng.copy(v_sb[:, 2 * i:2 * i + 2, :, 0:DH],
                             m_ps[:, :].rearrange("p (k h w) -> p k h w", k=2, h=H)).then_inc(v_copied, 1)

                def copy_heads(bb, g):
                    eng.wait_ge(pv_done, 12 * bb + 3 * (g + 1))
                    if g == 0:
                        wait_past(eng, full["o"], 4 * bb)
                    eng.copy(heads[:, g, :], o_ps[:, :]).then_inc(heads_copied, 1)

                def copy_at(qb):
                    eng.wait_ge(full["at"], 4 * (b - 1) + qb + 1)
                    wait_past(eng, full["fin"], 4 * (b - 1) + max(qb - 1, 0))
                    eng.copy(attnT[:, qb % 2, :, :], m_ps[:, 0:D].rearrange("p (c n) -> p c n", c=NC))\
                       .then_inc(at_copied, 1)

                for s in range(SLOTS):
                    if 3 in stages:
                        exp(s)
                    if 4 in stages and s == 2:
                        copy_heads(b - 1, NG - 1)
                    for slot, kind, k in work(stages):
                        if slot == s and kind in ("v", "at"):
                            {"v": copy_v, "at": copy_at}[kind](k)
                    if 3 in stages and s in (7, 12, 17):
                        copy_heads(b, s // 5 - 1)
                    if 1 in stages:
                        if s in (3, 10):
                            high(s // 10)
                        if s in (5, 12):
                            middle(s // 12)

            run(eng, iteration)

        @block.tensor
        def _(eng):
            eng.wait_ge(consts, 8)
            def turn_rows(i):
                for p in range(2):
                    eng.wait_ge(xn_done, 8 * i + 4 * (p + 1))
                    wait_past(eng, xnT_copied, 4 * i)
                    for c in range(NC):
                        for t in range(NQ):
                            mm = eng.transpose(st_ps[p][:, c * T + t * P:c * T + (t + 1) * P],
                                               xn[p][:, t, c * P:(c + 1) * P], ident[:, :])
                        mm.then_inc(xn_turned, 1)

            over_pairs(eng, turn_rows)
            eng.wait_ge(amax_done, NB + 3)
            eng.transpose(m_ps[0:2, 0:P], amax2[:, :], ident[:, :]).then_inc(amax_turned, 1)
            eng.wait_ge(wquant, 2)
            eng.matmul(m_ps[:, 0:2], ones2[:, :], amax_d[:, :], start=True, stop=True).then_inc(amax_turned, 1)
            eng.wait_ge(w_in, 16 * 8)
            eng.wait_ge(wquant, 12)
            eng.wait_ge(xnT_copied, 2 * NB)

            def iteration(b, par, stages):
                n = b + 1

                def scores(s):
                    g, u = divmod(s, 5)
                    if u == 0 and g % 2 == 0:
                        eng.wait_ge(shift_in[g // 2], 16 * (b + 1))
                    wait_past(eng, exp_done, SLOTS * b + s - 1)
                    for i, kb, col in unit_parts(u):
                        h = g * HG + i
                        mm = eng.matmul(st_ps[s % 2][:, col:col + T - kb * P],
                                        k_st[0:ROWS + SHIFT, par, h, kb * P:(kb + 1) * P],
                                        q_st[0:ROWS + SHIFT, par, h, kb * P:T], start=True, stop=True)
                    mm.then_inc(st_full, 1)

                def scores_for_max(e):
                    h, qb = divmod(e, NQ)
                    c = H * NQ * n + e
                    if e % (HG * NQ) == 0:
                        eng.wait_ge(stack_in[h // HG], 16 * 9 * (n + 1))
                    wait_past(eng, max_done, c - 1)
                    eng.matmul(s_ps[e % 2][:, 0:(qb + 1) * P], q_st[0:ROWS, 1 - par, h, qb * P:(qb + 1) * P],
                               k_st[0:ROWS, 1 - par, h, 0:(qb + 1) * P], start=True, stop=True)\
                       .then_inc(s_full, 1)

                def project(k):
                    w = (wq_sb, wk_sb)[k // 2]
                    for c in range(NC):
                        mm = eng.matmul(m_ps[:, :], w[:, c, k % 2, :], xnT[:, c, bass.ds((b + 2) * T, T)],
                                        start=(c == 0), stop=(c == NC - 1))
                    return mm

                def project_v(i):
                    if i == 0:
                        eng.wait_ge(xnv_in, 16 * (b + 1))
                    for t in range(2):
                        for c in range(NC):
                            mm = eng.matmul(m_ps[:, t * D:(t + 1) * D],
                                            xn_v[:, c, (2 * i + t) * P:(2 * i + t + 1) * P],
                                            wv_sb[:, c, :], start=(c == 0), stop=(c == NC - 1))
                    return mm

                def turn_heads(qb):
                    eng.wait_ge(heads_copied, 4 * b)
                    for g in range(NG):
                        mm = eng.transpose(m_ps[:, g * P:(g + 1) * P], heads[:, g, qb * P:(qb + 1) * P],
                                           ident[:, :])
                    return mm

                def turn_attn(qb):
                    eng.wait_ge(normed, 4 * (b - 1) + qb + 1)
                    for c in range(NC):
                        mm = eng.transpose(m_ps[:, c * P:(c + 1) * P], attn[:, qb, c * P:(c + 1) * P],
                                           ident[:, :])
                    return mm

                def outputs(qb):
                    eng.wait_ge(at_copied, 4 * (b - 1) + qb + 1)
                    for c in range(NC):
                        eng.matmul(m_ps[:, 0:D], attnT[:, qb % 2, c, :], wo_sb[:, c, :],
                                   start=(c == 0), stop=(c == NC - 1))
                    if qb == 0:
                        eng.wait_ge(xq_done, b)
                    for c in range(NC):
                        mm = eng.matmul(m_ps[:, D:2 * D], xq[:, c, qb * P:(qb + 1) * P], wf_q[:, c, :],
                                        start=(c == 0), stop=(c == NC - 1))
                    return mm

                def turn_max(i):
                    eng.wait_ge(max_done, H * NQ * n + H * NQ // 2 * (i + 1))
                    return eng.transpose(m_ps[0:H * NQ // 2, 0:P],
                                         rowmax[:, H * NQ // 2 * i:H * NQ // 2 * (i + 1)], ident[:, :])

                def pv(bb, g, step):
                    for kb in ((0,), (1, 3), (2,))[step]:
                        if kb == 0:
                            wait_past(eng, heads_copied, 4 * bb + g)
                            eng.wait_ge(v_copied, 2 * bb + 2)
                        eng.wait_ge(masked, SLOTS * bb + 5 * g + (2, 4, 5)[step])
                        for u in ((0, 1), (2, 3), (4,))[step]:
                            for i, k, col in unit_parts(u):
                                if k == kb:
                                    mm = eng.matmul(o_ps[32 * i:32 * i + 2 * DH, kb * P:T],
                                                    v_sb[:, kb, g * HG + i, :],
                                                    prob[u][:, col:col + T - kb * P],
                                                    start=(kb == 0), stop=(kb == 2),
                                                    skip_group_check=True)
                    mm.then_inc(pv_done, 1)

                def bank_free(prev):
                    _, kind, k = prev
                    s_, per = reader[kind]
                    eng.wait_ge(s_, per * (b + ahead[kind]) + k + 1)

                todo = work(stages)
                do = {"qk": project, "v": project_v, "o": turn_heads, "at": turn_attn, "fin": outputs,
                      "mt": turn_max}
                for s in range(SLOTS):
                    if 3 in stages:
                        scores(s)
                    if 2 in stages:
                        for e in range(FIRST_ITEM[s], FIRST_ITEM[s] + ITEMS[s]):
                            scores_for_max(e)
                    for at, item in enumerate(todo):
                        if item[0] != s:
                            continue
                        if at > 0:
                            bank_free(todo[at - 1])
                        elif isinstance(b, int) and b == -1:
                            eng.wait_ge(roped, 4)
                        elif isinstance(b, int) and b == 8:
                            eng.wait_ge(fin_done, 4 * 7)
                        else:
                            wait_past(eng, shift_done, 2 * (b + 1))
                        do[item[1]](item[2]).then_inc(full[item[1]], 1)
                    if 4 in stages and s < 2:
                        pv(b - 1, NG - 1, s + 1)
                    if 3 in stages:
                        for lag, step in ((3, 0), (5, 1), (6, 2)):
                            if s >= lag and (s - lag) % 5 == 0 and (s - lag) // 5 < NG:
                                pv(b, (s - lag) // 5, step)

            run(eng, iteration)


def kernel(L0_attn_X, L0_attn_W_q, L0_attn_W_k, L0_attn_W_v, L0_attn_W_o, L0_ffn_weight, L0_ffn_bias):
    import concourse.bacc as bacc
    from concourse.bass_utils import run_bass_kernel_spmd

    def turned(w):
        return np.ascontiguousarray(np.asarray(w).T)

    def pairs(w):
        return np.ascontiguousarray(np.asarray(w).reshape(H, J, 2, D).transpose(3, 2, 1, 0).reshape(D, 2, J * H))

    theta = (np.float32(10000.0) ** (np.float32(-2.0) * np.arange(J, dtype=np.float32) / np.float32(DH)))
    angles = (np.arange(T, dtype=np.float32)[:, None] * theta.astype(np.float32)[None, :]).T
    cos = np.ascontiguousarray(np.repeat(np.cos(angles), H, axis=0).astype(np.float32))
    sin = np.ascontiguousarray(np.repeat(np.sin(angles), H, axis=0).astype(np.float32))

    arrays = {"x": np.ascontiguousarray(np.asarray(L0_attn_X)), "wq": pairs(L0_attn_W_q), "wk": pairs(L0_attn_W_k),
              "wv": turned(L0_attn_W_v), "wo": turned(L0_attn_W_o), "wf": turned(L0_ffn_weight),
              "bias": np.ascontiguousarray(np.asarray(L0_ffn_bias)), "cos": cos, "sin": sin}
    nc = bacc.Bacc("TRN2", target_bir_lowering=False, num_devices=1)
    args = [nc.dram_tensor(f"{k}_dram", a.shape, F32, kind="ExternalInput").ap() for k, a in arrays.items()]
    args.append(nc.dram_tensor("out_dram", (NB, T, D), F32, kind="ExternalOutput").ap())
    attention_ffn_block(nc, *args)
    r = run_bass_kernel_spmd(nc, [{f"{k}_dram": a for k, a in arrays.items()}], core_ids=[0])
    return r.results[0]["out_dram"]
```

```python
from contextlib import ExitStack

import numpy as np

import concourse.bass as bass
from concourse import mybir

F32 = mybir.dt.float32
BF16 = mybir.dt.bfloat16
U32 = mybir.dt.uint32
ALU = mybir.AluOpType
ACT = mybir.ActivationFunctionType
AX = mybir.AxisListType

P = 128
NB, T, D = 8, 512, 256
H, DH = 16, 16
J = DH // 2
NQ = T // P
NC = D // P
HG = 4
NG = H // HG
SLOTS = 5 * NG
PAIR = 2 * T
SCALE = float(DH) ** -0.5
EPS = 1e-5
FP8_MAX = 448.0
NEG = -3.0e38
Q_PARTS = ((0, 1), (0, 1, 2), (0,))
K_PARTS = ((0, 1, 2), (0,), (0, 1))
ROWS = 6 * DH
SHIFT = 2

MAX_BANKS = [[(0, 3, 0)], [(0, 0, 0), (0, 2, P)], [(1, 3, 0)], [(1, 0, 0), (1, 2, P)], [(0, 1, 0), (1, 1, 2 * P)]]
BANKS = H // 2 * len(MAX_BANKS)
ITEMS = H * NQ
ITEMS_UP_TO = [sum(len(MAX_BANKS[i % len(MAX_BANKS)]) for i in range(f + 1)) for f in range(BANKS)]
assert BANKS == 2 * SLOTS and ITEMS_UP_TO[-1] == ITEMS

MISC = [(0, "mt", 1), (0, "qk", 0), (1, "v", 0), (2, "qk", 1), (4, "v", 1), (4, "o", 0),
        (5, "qk", 2), (6, "o", 1), (7, "qk", 3), (8, "o", 2), (8, "o", 3), (10, "at", 0), (11, "mt", 0),
        (12, "fin", 0), (13, "at", 1), (14, "fin", 1), (15, "at", 2), (16, "fin", 2), (17, "at", 3),
        (19, "fin", 3)]
SHARED_BANK = {(kind, k): i % 2 for i, (_, kind, k) in enumerate(MISC)}


HALVES = 2 * SLOTS
ST_BANK = [i % 3 for i in range(HALVES - 1)] + [1]
ST_BEFORE = [max(j for j in range(-HALVES, i) if ST_BANK[j % HALVES] == ST_BANK[i]) for i in range(HALVES)]


def wait_past(eng, sem, count):
    if not (isinstance(count, int) and count <= 0):
        eng.wait_ge(sem, count)


def over_pairs(eng, body):
    body(0)
    with eng.Fori(1, NB // 2) as i:
        body(i)


def unit_parts(u, half):
    if u < 2:
        return [(2 * u + half, 0, 0)]
    if u < 4:
        return [(2 * (u - 2) + half, 3, 0), (2 * (u - 2) + half, 1, P)]
    return [(2 * half + i, 2, 2 * P * i) for i in range(2)]


def attention_ffn_block(nc, x, wq, wk, wv, wo, wf, bias, cos, sin, out):
    with ExitStack() as ctx:
        def sb(name, shape, dt=F32):
            return ctx.enter_context(nc.sbuf_tensor(name, shape, dt))

        def pb(name, shape):
            return ctx.enter_context(nc.psum_tensor(name, shape, F32))

        def sem(name):
            return ctx.enter_context(nc.semaphore(name))

        wq_sb = sb("wq_sb", [P, NC, 2, P])
        wk_sb = sb("wk_sb", [P, NC, 2, P])
        wv_sb = sb("wv_sb", [P, NC, D])
        wo_sb = sb("wo_sb", [P, NC, D])
        wf_sb = sb("wf_sb", [P, NC, D])
        wf_q = sb("wf_q", [P, NC, D], BF16)
        bias_sb = sb("bias_sb", [P, D])
        cos_sb = sb("cos_sb", [P, T])
        sin_sb = sb("sin_sb", [P, T])
        ident = sb("ident", [P, P])
        ones2 = sb("ones2", [2, P])
        causal = sb("causal", [P, T])
        xnT = sb("xnT", [P, NC, NB * T])
        xn_v = sb("xn_v", [P, NC, T])
        q_st = sb("q_st", [P, 2, H, T], BF16)
        k_st = sb("k_st", [P, 2, H, T], BF16)
        v_sb = sb("v_sb", [P, NQ, H, 2 * DH])
        prob = [sb(f"prob{u}", [P, PAIR]) for u in range(5)]
        heads = sb("heads", [P, NG, T])
        prod = sb("prod", [P, 4, T])
        rot = sb("rot", [P, 2, T])
        rem = sb("rem", [P, 2, T])
        parts = sb("parts", [P, 2, 3, 2, T], BF16)
        scratch = sb("scratch", [P, 2, T], BF16)
        rowmax = sb("rowmax", [P, H * NQ])
        shift = sb("shift", [H * NQ // 2, SHIFT, P], BF16)
        rden = sb("rden", [P, H])
        attn = sb("attn", [P, NQ, D])
        attnT = sb("attnT", [P, 2, NC, P])
        x_res = sb("x_res", [P, NQ, D])
        xq = sb("xq", [P, NC, T], BF16)
        stats = sb("stats", [P, 2, NQ, 6])
        mv_b = sb("mv_b", [P, 2, NQ, 2])
        mv = sb("mv", [P, NB * NQ, 2])
        ve = sb("ve", [P, NB * NQ])
        half = sb("half", [P, NB * NQ])
        rstd = sb("rstd", [P, NB * NQ])
        amax = sb("amax", [P, NB + 1])
        amax2 = sb("amax2", [P, 2])
        amax_r = sb("amax_r", [2, 1])
        amax_d = sb("amax_d", [2, 2])
        amax_b = sb("amax_b", [P, 2])
        inv = sb("inv", [P, 2])
        scale = sb("scale", [P, 2])
        unscale = sb("unscale", [P, 2])
        both = sb("both", [P, 1])
        x_all = q_st[:, :, :, :].rearrange("p a h t -> p (a h t)").bitcast(F32).rearrange(
            "p (b n d) -> p b n d", b=NB, n=NQ)
        xn = [prob[i][:, :].rearrange("p (n d) -> p n d", n=NQ) for i in range(2)]
        qv = sb("qv", [P, NC * T])
        qe = sb("qe", [P, NC * T])

        st_ps = [pb(f"st_ps{i}", [P, T]) for i in range(3)]
        s_ps = [pb(f"s_ps{i}", [P, T]) for i in range(2)]
        o_ps = pb("o_ps", [P, T])
        m_ps = [pb(f"m_ps{i}", [P, T]) for i in range(2)]
        shared = {(kind, k): m_ps[bank] for (kind, k), bank in SHARED_BANK.items()}

        turn_ps = [[st_ps[0], st_ps[1]], [st_ps[2], o_ps]]

        qk_dram = nc.dram_tensor("qk_parts", [2, 2, 3, 2, J, H, T], BF16, kind="Internal").ap()
        shift_dram = nc.dram_tensor("shift_rows", [2, SHIFT, H * NQ // 2, P], BF16, kind="Internal").ap()

        w_in = sem("w_in")
        x_in = [sem(f"x_in{i}") for i in range(2)]
        xnv_in = sem("xnv_in")
        res_in = sem("res_in")
        parts_out = sem("parts_out")
        stack_in = [sem(f"stack_in{g}") for g in range(NG)]
        shift_out = [sem(f"shift_out{i}") for i in range(2)]
        shift_in = [sem(f"shift_in{i}") for i in range(2)]
        y_out = sem("y_out")
        consts = sem("consts")
        ln_stat = sem("ln_stat")
        ln_agg = sem("ln_agg")
        ln_mv = sem("ln_mv")
        ln_ve = sem("ln_ve")
        ln_rstd = sem("ln_rstd")
        xn_done = sem("xn_done")
        xn_turned = sem("xn_turned")
        xnT_copied = sem("xnT_copied")
        amax_done = sem("amax_done")
        amax_turned = sem("amax_turned")
        wquant = sem("wquant")
        st_full = sem("st_full")
        s_full = sem("s_full")
        full = {k: sem(f"{k}_full") for k in ("qk", "v", "o", "at", "fin", "mt")}
        pv_done = sem("pv_done")
        exp_done = sem("exp_done")
        max_done = sem("max_done")
        roped = sem("roped")
        v_copied = sem("v_copied")
        heads_copied = sem("heads_copied")
        recip_done = sem("recip_done")
        normed = sem("normed")
        at_copied = sem("at_copied")
        fin_done = sem("fin_done")
        shift_hi = sem("shift_hi")
        shift_done = sem("shift_done")
        masked = sem("masked")
        max_begun = sem("max_begun")
        mask_begun = sem("mask_begun")
        agg_begun = sem("agg_begun")
        rotated = sem("rotated")
        hi_done = sem("hi_done")
        rem_done = sem("rem_done")
        mid_done = sem("mid_done")
        low_done = sem("low_done")
        qv_done = sem("qv_done")
        qe_done = sem("qe_done")
        qc_done = sem("qc_done")
        qw_done = sem("qw_done")
        xq_done = sem("xq_done")
        res_done = sem("res_done")

        reader = {"qk": (roped, 4), "v": (v_copied, 2), "o": (normed, 4), "at": (at_copied, 4),
                  "fin": (fin_done, 4), "mt": (shift_done, 2)}
        ahead = {"qk": (2,) * 4, "v": (0,) * 2, "o": (-1,) * 4, "at": (-1,) * 4, "fin": (-1,) * 4, "mt": (1, 0)}

        def work(stages):
            stage_of = {2: 1, 1: 2, 0: 3, -1: 4}
            return [(s, kind, k) for s, kind, k in MISC if stage_of[ahead[kind][k]] in stages]

        block = ctx.enter_context(nc.Block())

        LOOP = (2, 6)

        def run(eng, iteration):
            every = {1, 2, 3, 4}
            iteration(-2, 0, {1}, set())
            iteration(-1, 1, {1, 2}, {1})
            iteration(0, 0, {1, 2, 3}, {1, 2})
            iteration(1, 1, every, {1, 2, 3})
            with eng.Fori(0, (LOOP[1] - LOOP[0]) // 2) as i:
                iteration(2 * i + LOOP[0], 0, every, every)
                iteration(2 * i + LOOP[0] + 1, 1, every, every)
            iteration(6, 0, {2, 3, 4}, every)
            iteration(7, 1, {3, 4}, {2, 3, 4})
            iteration(8, 0, {4}, {3, 4})

        @block.sync
        def _(eng):
            for dst, src in ((wq_sb, wq), (wk_sb, wk)):
                eng.dma_start(dst[:, :, :, :], src.rearrange("(c p) r m -> p c r m", p=P)).then_inc(w_in, 16)
            for dst, src in ((wv_sb, wv), (wo_sb, wo), (wf_sb, wf)):
                eng.dma_start(dst[:, :, :], src.rearrange("(c p) n -> p c n", p=P)).then_inc(w_in, 16)
            eng.dma_start(cos_sb[:, :], cos).then_inc(w_in, 16)
            eng.dma_start(sin_sb[:, :], sin).then_inc(w_in, 16)
            eng.dma_start(bias_sb[:, :], bias.partition_broadcast(P)).then_inc(w_in, 16)
            def load_x(i):
                for p in range(2):
                    wait_past(eng, x_in[p], 16 * i)
                    eng.dma_start(x_all[:, bass.ds(2 * i + p, 1)].rearrange("p a n d -> p (a n) d"),
                                  x[bass.ds(2 * i + p, 1)].rearrange("a (n p) d -> p (a n) d", p=P))\
                       .then_inc(x_in[p], 16)

            over_pairs(eng, load_x)
            eng.wait_ge(xnT_copied, 2 * NB)
            eng.dma_start(xn_v[:, :, :], xnT[:, :, 0:T]).then_inc(xnv_in, 16)

            def iteration(b, par, stages, before):
                if 3 in stages:
                    shift_rows(b, par, 1)
                if 4 in stages:
                    wait_past(eng, y_out, 16 * (b - 1))
                    eng.dma_start(x_res[:, :, :], x[bass.ds(b - 1, 1)].rearrange("a (n p) d -> p (a n) d", p=P))\
                       .then_inc(res_in, 16)
                if 3 in stages and 2 in stages:
                    eng.wait_ge(full["v"], 2 * (b + 1))
                    eng.dma_start(xn_v[:, :, :], xnT[:, :, bass.ds((b + 1) * T, T)]).then_inc(xnv_in, 16)
                if 1 in stages:
                    n = b + 2
                    eng.wait_ge(low_done, 2 * n + 1)
                    eng.dma_start(qk_view(par, 0),
                                  parts[:, 0].rearrange("p t r n -> p (t r) n")).then_inc(parts_out, 16)
                    eng.wait_ge(parts_out, 32 * n + 16)
                    for g in range(2):
                        read_stack(b, par, g, "q", 3 in stages)
                if 2 in stages:
                    shift_rows(b + 1, 1 - par, 0)
                if 1 in stages:
                    eng.wait_ge(low_done, 2 * n + 2)
                    eng.dma_start(qk_view(par, 1),
                                  parts[:, 1].rearrange("p t r n -> p (t r) n")).then_inc(parts_out, 16)
                    eng.wait_ge(parts_out, 32 * n + 32)
                    for g in range(NG):
                        read_stack(b, par, g, "k", 3 in stages)
                        if g >= 2:
                            read_stack(b, par, g, "q", False)
                if 4 in stages:
                    eng.wait_ge(fin_done, 4 * b)
                    eng.dma_start(out[bass.ds(b - 1, 1)].rearrange("a (n p) d -> p (a n) d", p=P),
                                  x_res[:, :, :]).then_inc(y_out, 16)

            def qk_view(par, which):
                return qk_dram[par, which].rearrange("t r j h n -> (j h) (t r) n")

            def read_stack(b, par, g, which, busy):
                if busy:
                    eng.wait_ge(st_full, HALVES * b + 10 * (g + 1))
                h0 = g * HG
                dst, runs, w = (q_st, Q_PARTS, 0) if which == "q" else (k_st, K_PARTS, 1)
                src = qk_dram[par, w].rearrange("t r j h n -> (t r j) h n")
                row = 0
                for run_ in runs:
                    rows = DH * len(run_)
                    eng.dma_start(dst[row:row + rows, par, h0:h0 + HG, :],
                                  src[DH * run_[0]:DH * run_[0] + rows, h0:h0 + HG, :]).then_inc(stack_in[g], 16)
                    row += rows

            def shift_rows(n, par, half_):
                eng.wait_ge(shift_done, 2 * n + half_ + 1)
                eng.dma_start(shift_dram[half_].rearrange("t a n -> a t n"), shift[:, :, :])\
                   .then_inc(shift_out[half_], 16)
                eng.wait_ge(shift_out[half_], 16 * (n + 1))
                h0 = half_ * (H // 2)
                eng.dma_start(q_st[ROWS:ROWS + SHIFT, par, h0:h0 + H // 2, :],
                              shift_dram[half_].rearrange("t a n -> t (a n)").rearrange(
                                  "t (h n) -> t h n", h=H // 2)).then_inc(shift_in[half_], 16)

            run(eng, iteration)
            eng.wait_ge(y_out, 16 * NB)

        @block.gpsimd
        def _(eng):
            eng.memset(ident[:, :], 0.0).then_inc(consts, 1)
            eng.memset(causal[:, :], 0.0).then_inc(consts, 1)
            eng.memset(ones2[:, :], 1.0).then_inc(consts, 1)
            eng.memset(half[:, :], -0.5).then_inc(consts, 1)
            eng.memset(v_sb[:, :, :, :], 1.0).then_inc(consts, 1)
            eng.wait_ge(consts, 5)
            eng.memset(k_st[ROWS:ROWS + SHIFT, :, :, :].rearrange("p a h t -> p (a h t)").bitcast(F32),
                       float(np.array([0x3F803F80], np.uint32).view(np.float32)[0])).then_inc(consts, 1)
            eng.wait_ge(consts, 6)
            eng.affine_select(out=ident[:, :], in_=ident[:, :], compare_op=ALU.not_equal, fill=1.0,
                              base=0, pattern=[[-1, P]], channel_multiplier=1).then_inc(consts, 1)
            eng.affine_select(out=causal[:, T - P:T], in_=causal[:, T - P:T], compare_op=ALU.is_ge, fill=NEG,
                              base=0, pattern=[[-1, P]], channel_multiplier=1).then_inc(consts, 1)
            eng.wait_ge(ln_ve, 1)
            eng.tensor_tensor(rstd[:, :], ve[:, :], half[:, :], ALU.pow).then_inc(ln_rstd, 1)

            def iteration(b, par, stages, before):
                n = b + 2

                def mask(s):
                    u = s % 5
                    if u < 2:
                        ap, pat = prob[u].rearrange("p (h q) -> p h q", h=2)[:, :, 0:P], [[0, 2], [1, P]]
                    elif u < 4:
                        ap = prob[u].rearrange("p (h q) -> p h q", h=2)[:, :, 0:2 * P]
                        pat = [[0, 2], [0, 2], [1, P]]
                    else:
                        ap, pat = prob[u].rearrange("p (h q) -> p h q", h=4)[:, :, 0:P], [[0, 4], [1, P]]
                    eng.wait_ge(exp_done, HALVES * b + 2 * (s + 1))
                    eng.sem_inc(mask_begun)
                    eng.affine_select(out=ap, in_=ap, compare_op=ALU.is_ge, fill=0.0, base=0,
                                      pattern=pat, channel_multiplier=-1).then_inc(masked, 1)

                def rotate(w):
                    eng.wait_ge(roped, 4 * n + 2 * w + 2)
                    wait_past(eng, rem_done, 2 * n + w)
                    eng.tensor_tensor(rot[:, 0, :], prod[:, 0, :], prod[:, 2, :], ALU.subtract).then_inc(rotated, 1)
                    eng.tensor_tensor(rot[:, 1, :], prod[:, 1, :], prod[:, 3, :], ALU.add).then_inc(rotated, 1)

                def remainder(w):
                    eng.wait_ge(rotated, 4 * n + 2 * w + 2)
                    eng.wait_ge(hi_done, 2 * n + w + 1)
                    wait_past(eng, low_done, 2 * n + w)
                    eng.tensor_tensor(rem[:, :, :], rot[:, :, :], parts[:, w, 0], ALU.subtract).then_inc(rem_done, 1)

                def low(w):
                    eng.wait_ge(mid_done, 2 * n + w + 1)
                    eng.tensor_tensor(parts[:, w, 2], rem[:, :, :], parts[:, w, 1], ALU.subtract).then_inc(low_done, 1)

                for s in range(SLOTS):
                    if 3 in stages:
                        mask(s)
                    if 1 in stages:
                        if s in (3, 8):
                            rotate(s // 8)
                        if s in (6, 11):
                            remainder(s // 11)
                        if s in (9, 14):
                            low(s // 14)
                    if 4 in stages:
                        if s == 7:
                            eng.wait_ge(res_in, 16 * b)
                            eng.tensor_tensor(x_res[:, :, :], x_res[:, :, :],
                                              bias_sb[:, None, :].to_broadcast([P, NQ, D]), ALU.add)\
                               .then_inc(res_done, 1)
                        if s == 4:
                            eng.wait_ge(qc_done, b)
                            eng.tensor_tensor(qv[:, :], qv[:, :], qe[:, :], ALU.add).then_inc(qw_done, 1)
                        if s == 5:
                            eng.wait_ge(qw_done, b)
                            wait_past(eng, full["fin"], 4 * (b - 1))
                            eng.tensor_tensor(xq.rearrange("p c t -> p (c t)"), qv[:, :], qe[:, :],
                                              ALU.subtract).then_inc(xq_done, 1)

            eng.wait_ge(w_in, 16 * 8)
            run(eng, iteration)

        @block.vector
        def _(eng):
            with eng.Fori(0, NB // 2) as i:
                for p in range(2):
                    eng.wait_ge(x_in[p], 16 * (i + 1))
                    for t in range(NQ):
                        eng.bn_stats(stats[:, p, t, :],
                                     x_all[:, bass.ds(2 * i + p, 1), t, :].rearrange("p a d -> p (a d)"))\
                           .then_inc(ln_stat, 1)
                    eng.wait_ge(ln_stat, 8 * i + 4 * (p + 1))
                    eng.sem_inc(agg_begun)
                    for t in range(NQ):
                        eng.bn_aggr(mv_b[:, p, t, :], stats[:, p, t, :]).then_inc(ln_agg, 1)
                    eng.wait_ge(ln_agg, 8 * i + 4 * (p + 1))
                    eng.tensor_copy(mv[:, bass.ds((2 * i + p) * NQ, NQ), :], mv_b[:, p, :, :]).then_inc(ln_mv, 1)
            eng.wait_ge(ln_mv, NB)
            eng.tensor_scalar(ve[:, :], mv[:, :, 1], EPS, None, ALU.add).then_inc(ln_ve, 1)
            eng.wait_ge(ln_rstd, 1)
            def normalise(i):
                for p in range(2):
                    if p == 0:
                        wait_past(eng, xn_turned, 4 * i - 2)
                    else:
                        wait_past(eng, xn_turned, 4 * i)
                    for t in range(NQ):
                        row = (2 * i + p) * NQ + t
                        eng.tensor_scalar(xn[p][:, t, :],
                                          x_all[:, bass.ds(2 * i + p, 1), t, :].rearrange("p a d -> p (a d)"),
                                          mv[:, bass.ds(row, 1), 0], rstd[:, bass.ds(row, 1)],
                                          ALU.subtract, ALU.mult).then_inc(xn_done, 1)
                    eng.wait_ge(xn_done, 8 * i + 4 * (p + 1))
                    eng.tensor_reduce(amax[:, bass.ds(2 * i + p, 1)], xn[p], AX.XY, ALU.max,
                                      apply_absolute_value=True).then_inc(amax_done, 1)

            over_pairs(eng, normalise)
            eng.wait_ge(w_in, 16 * 8)
            eng.tensor_reduce(amax[:, NB:NB + 1], wf_sb[:, :, :], AX.XY, ALU.max,
                              apply_absolute_value=True).then_inc(amax_done, 1)
            eng.wait_ge(amax_done, NB + 1)
            eng.tensor_reduce(amax2[:, 0:1], amax[:, 0:NB], AX.X, ALU.max).then_inc(amax_done, 1)
            eng.tensor_copy(amax2[:, 1:2], amax[:, NB:NB + 1]).then_inc(amax_done, 1)
            eng.wait_ge(amax_turned, 1)
            eng.tensor_reduce(amax_r[:, :], m_ps[0][0:2, 0:P], AX.X, ALU.max).then_inc(wquant, 1)
            eng.wait_ge(consts, 8)
            eng.wait_ge(wquant, 1)
            eng.tensor_scalar(amax_d[:, :], ident[0:2, 0:2], amax_r[:, 0:1], None, ALU.mult).then_inc(wquant, 1)
            eng.wait_ge(amax_turned, 2)
            eng.tensor_scalar(amax_b[:, :], m_ps[0][:, 0:2], 1e-12, None, ALU.max).then_inc(wquant, 1)
            eng.wait_ge(wquant, 3)
            eng.reciprocal(inv[:, :], amax_b[:, :]).then_inc(wquant, 1)
            eng.tensor_scalar(unscale[:, :], amax_b[:, :], 1.0 / FP8_MAX, None, ALU.mult).then_inc(wquant, 1)
            eng.wait_ge(wquant, 5)
            eng.tensor_scalar(scale[:, :], inv[:, :], FP8_MAX, None, ALU.mult).then_inc(wquant, 1)
            eng.tensor_tensor(both[:, :], unscale[:, 0:1], unscale[:, 1:2], ALU.mult).then_inc(wquant, 1)
            eng.wait_ge(wquant, 7)
            nw = NC * D
            wf_f = wf_sb[:, :, :].rearrange("p c n -> p (c n)")
            eng.tensor_scalar(qv[:, 0:nw], wf_f, scale[:, 1:2], None, ALU.mult).then_inc(wquant, 1)
            eng.wait_ge(wquant, 8)
            eng.tensor_scalar(qe[:, 0:nw].bitcast(U32), qv[:, 0:nw].bitcast(U32), 0x7F800000, None,
                              ALU.bitwise_and).then_inc(wquant, 1)
            eng.wait_ge(wquant, 9)
            eng.tensor_scalar(qe[:, 0:nw], qe[:, 0:nw], 2.0 ** -6, 1.5 * 2.0 ** 20, ALU.max, ALU.mult)\
               .then_inc(wquant, 1)
            eng.wait_ge(wquant, 10)
            eng.tensor_tensor(qv[:, 0:nw], qv[:, 0:nw], qe[:, 0:nw], ALU.add).then_inc(wquant, 1)
            eng.wait_ge(wquant, 11)
            eng.tensor_tensor(wf_q[:, :, :].rearrange("p c n -> p (c n)"), qv[:, 0:nw], qe[:, 0:nw],
                              ALU.subtract).then_inc(wquant, 1)
            eng.tensor_scalar(wo_sb[:, :, :], wo_sb[:, :, :], scale[:, 0:1], scale[:, 1:2], ALU.mult, ALU.mult)\
               .then_inc(wquant, 1)
            eng.wait_ge(wquant, 13)

            def iteration(b, par, stages, before):
                def row_max(f):
                    pair, m = divmod(f, len(MAX_BANKS))
                    eng.wait_ge(s_full, BANKS * (b + 1) + f + 1)
                    if f == 0:
                        wait_past(eng, full["mt"], 2 * b + 1)
                    if f == BANKS // 2:
                        wait_past(eng, full["mt"], 2 * b + 2)
                    eng.sem_inc(max_begun)
                    for h, qb, col in MAX_BANKS[m]:
                        e = (2 * pair + h) * NQ + qb
                        w = P * (qb + 1)
                        eng.tensor_tensor_reduce(scratch[:, f % 2, col:col + w], s_ps[f % 2][:, col:col + w],
                                                 causal[:, T - w:T], 1.0, NEG, ALU.add, ALU.max,
                                                 rowmax[:, e:e + 1]).then_inc(max_done, 1)

                def rope(k):
                    bank = shared["qk", k]
                    n = b + 2
                    r = k % 2
                    eng.wait_ge(full["qk"], 4 * n + k + 1)
                    if r == 0:
                        wait_past(eng, rotated, 4 * n + k)
                    a, c = (prod[:, 0, :], prod[:, 1, :]) if r == 0 else (prod[:, 3, :], prod[:, 2, :])
                    eng.tensor_tensor(a, bank[:, :], cos_sb[:, :], ALU.mult)
                    eng.tensor_tensor(c, bank[:, :], sin_sb[:, :], ALU.mult).then_inc(roped, 1)

                def norm(qb):
                    bank = shared["o", qb]
                    o = bank[:, :].rearrange("p (h w) -> p h w", h=H)
                    eng.wait_ge(full["o"], 4 * (b - 1) + qb + 1)
                    wait_past(eng, normed, 4 * (b - 1) + qb)
                    eng.reciprocal(rden[:, :, None], o[:, :, DH:DH + 1]).then_inc(recip_done, 1)
                    eng.wait_ge(recip_done, 4 * (b - 1) + qb + 1)
                    if qb == 0:
                        wait_past(eng, full["at"], 4 * (b - 1))
                    eng.tensor_tensor(attn[:, qb, :].rearrange("p (h w) -> p h w", h=H), o[:, :, 0:DH],
                                      rden[:, :, None].to_broadcast([P, H, DH]), ALU.mult).then_inc(normed, 1)

                def finish(qb):
                    bank = shared["fin", qb]
                    eng.wait_ge(full["fin"], 4 * (b - 1) + qb + 1)
                    if qb == 0:
                        eng.wait_ge(res_done, b)
                    eng.scalar_tensor_tensor(out=x_res[:, qb, :], in0=bank[:, 0:D], scalar=both[:, 0:1],
                                             in1=x_res[:, qb, :], op0=ALU.mult, op1=ALU.add)\
                       .then_inc(fin_done, 1)

                def split_max(i):
                    bank = shared["mt", i]
                    n = b + ahead["mt"][i]
                    c = 2 * n + i
                    rows = H * NQ // 2
                    eng.wait_ge(full["mt"], c + 1)
                    wait_past(eng, shift_out[1 - i], 16 * (n + i))
                    eng.tensor_scalar(shift[:, 0, :], bank[0:rows, 0:P], -1.0, None, ALU.mult).then_inc(shift_hi, 1)
                    eng.wait_ge(shift_hi, c + 1)
                    eng.scalar_tensor_tensor(out=shift[:, 1, :], in0=bank[0:rows, 0:P], scalar=-1.0,
                                             in1=shift[:, 0, :], op0=ALU.mult, op1=ALU.subtract)\
                       .then_inc(shift_done, 1)

                for s in range(SLOTS):
                    if 2 in stages:
                        row_max(2 * s)
                    for slot, kind, k in work(stages):
                        if slot == s and kind in ("qk", "o", "fin", "mt"):
                            {"qk": rope, "o": norm, "fin": finish, "mt": split_max}[kind](k)
                    if 2 in stages:
                        row_max(2 * s + 1)
                    if s == 1 and 4 in stages:
                        eng.wait_ge(qv_done, b)
                        eng.tensor_scalar(qe[:, :].bitcast(U32), qv[:, :].bitcast(U32), 0x7F800000, None,
                                          ALU.bitwise_and).then_inc(qe_done, 1)
                    if s == 3 and 4 in stages:
                        eng.wait_ge(qe_done, b)
                        eng.tensor_scalar(qe[:, :], qe[:, :], 2.0 ** -6, 1.5 * 2.0 ** 20, ALU.max, ALU.mult)\
                           .then_inc(qc_done, 1)

            run(eng, iteration)

        @block.scalar
        def _(eng):
            with eng.Fori(0, NB // 2) as i:
                for p in range(2):
                    for c in range(NC):
                        eng.wait_ge(xn_turned, 4 * i + 2 * p + c + 1)
                        eng.copy(xnT[:, c, bass.ds((2 * i + p) * T, T)], turn_ps[p][c][:, :])\
                           .then_inc(xnT_copied, 1)
            eng.wait_ge(consts, 8)
            eng.wait_ge(wquant, 13)

            def iteration(b, par, stages, before):
                n = b + 2

                def high(w):
                    eng.wait_ge(rotated, 4 * n + 2 * w + 2)
                    wait_past(eng, parts_out, 32 * n)
                    eng.copy(parts[:, w, 0], rot[:, :, :]).then_inc(hi_done, 1)

                def middle(w):
                    eng.wait_ge(rem_done, 2 * n + w + 1)
                    eng.copy(parts[:, w, 1], rem[:, :, :]).then_inc(mid_done, 1)

                def exp(s):
                    g, u = divmod(s, 5)
                    if g > 0 or not isinstance(b, int) or b > 0:
                        eng.wait_ge(pv_done, 12 * b + 3 * (g - 1) + (1, 1, 2, 2, 3)[u])
                    for half in range(2):
                        eng.wait_ge(st_full, 2 * (SLOTS * b + s) + half + 1)
                        eng.activation(prob[u][:, half * T:(half + 1) * T], st_ps[ST_BANK[2 * s + half]][:, :],
                                       ACT.Exp, scale=SCALE).then_inc(exp_done, 1)

                def copy_v(i):
                    bank = shared["v", i]
                    eng.wait_ge(full["v"], 2 * b + i + 1)
                    if i == 0:
                        wait_past(eng, pv_done, 12 * b)
                    eng.copy(v_sb[:, 2 * i:2 * i + 2, :, 0:DH],
                             bank[:, :].rearrange("p (k h w) -> p k h w", k=2, h=H)).then_inc(v_copied, 1)

                def copy_heads(bb, g):
                    eng.wait_ge(pv_done, 12 * bb + 3 * (g + 1))
                    if g == 0:
                        wait_past(eng, full["o"], 4 * bb)
                    eng.copy(heads[:, g, :], o_ps[:, :]).then_inc(heads_copied, 1)

                def copy_at(qb):
                    bank = shared["at", qb]
                    eng.wait_ge(full["at"], 4 * (b - 1) + qb + 1)
                    wait_past(eng, full["fin"], 4 * (b - 1) + max(qb - 1, 0))
                    eng.copy(attnT[:, qb % 2, :, :], bank[:, 0:D].rearrange("p (c n) -> p c n", c=NC))\
                       .then_inc(at_copied, 1)

                for s in range(SLOTS):
                    if 3 in stages:
                        exp(s)
                    if 4 in stages and s == 0:
                        wait_past(eng, xq_done, b - 1)
                        eng.mul(qv[:, :].rearrange("p (c t) -> p c t", c=NC),
                                xnT[:, :, bass.ds((b - 1) * T, T)], scale[:, 0:1]).then_inc(qv_done, 1)
                    if 4 in stages and s == 2:
                        copy_heads(b - 1, NG - 1)
                    for slot, kind, k in work(stages):
                        if slot == s and kind in ("v", "at"):
                            {"v": copy_v, "at": copy_at}[kind](k)
                    if 3 in stages and s in (7, 12, 17):
                        copy_heads(b, s // 5 - 1)
                    if 1 in stages:
                        if s in (5, 10):
                            high(s // 10)
                        if s in (8, 13):
                            middle(s // 13)

            run(eng, iteration)

        @block.tensor
        def _(eng):
            eng.wait_ge(consts, 8)
            def turn_rows(i):
                for p in range(2):
                    eng.wait_ge(xn_done, 8 * i + 4 * (p + 1))
                    wait_past(eng, xnT_copied, 4 * i)
                    for c in range(NC):
                        for t in range(NQ):
                            mm = eng.transpose(turn_ps[p][c][:, t * P:(t + 1) * P],
                                               xn[p][:, t, c * P:(c + 1) * P], ident[:, :])
                        mm.then_inc(xn_turned, 1)

            over_pairs(eng, turn_rows)
            eng.wait_ge(amax_done, NB + 3)
            eng.transpose(m_ps[0][0:2, 0:P], amax2[:, :], ident[:, :]).then_inc(amax_turned, 1)
            eng.wait_ge(wquant, 2)
            eng.matmul(m_ps[0][:, 0:2], ones2[:, :], amax_d[:, :], start=True, stop=True).then_inc(amax_turned, 1)
            eng.wait_ge(w_in, 16 * 8)
            eng.wait_ge(wquant, 13)
            eng.wait_ge(xnT_copied, 2 * NB)

            def iteration(b, par, stages, before):
                n = b + 1

                def scores(s):
                    g, u = divmod(s, 5)
                    if u == 0 and g % 2 == 0:
                        eng.wait_ge(shift_in[g // 2], 16 * (b + 1))
                    for half in range(2):
                        i = 2 * s + half
                        wait_past(eng, exp_done, HALVES * b + ST_BEFORE[i] + 1)
                        for j, kb, col in unit_parts(u, half):
                            h = g * HG + j
                            mm = eng.matmul(st_ps[ST_BANK[i]][:, col:col + T - kb * P],
                                            k_st[0:ROWS + SHIFT, par, h, kb * P:(kb + 1) * P],
                                            q_st[0:ROWS + SHIFT, par, h, kb * P:T], start=True, stop=True)
                        mm.then_inc(st_full, 1)
                        if half == 0 and 2 in stages:
                            scores_for_max(2 * s)

                def scores_for_max(f):
                    pair, m = divmod(f, len(MAX_BANKS))
                    if f % (BANKS // NG) == 0:
                        g = f // (BANKS // NG)
                        eng.wait_ge(stack_in[g], 16 * 6 * (n + 1))
                    wait_past(eng, max_done, ITEMS * n + (ITEMS_UP_TO[f - 2] if f >= 2 else ITEMS_UP_TO[f - 2] - ITEMS))
                    for i, qb, col in MAX_BANKS[m]:
                        h = 2 * pair + i
                        mm = eng.matmul(s_ps[f % 2][:, col:col + (qb + 1) * P],
                                        q_st[0:ROWS, 1 - par, h, qb * P:(qb + 1) * P],
                                        k_st[0:ROWS, 1 - par, h, 0:(qb + 1) * P], start=True, stop=True)
                    mm.then_inc(s_full, 1)

                def project(k):
                    bank = shared["qk", k]
                    w = (wq_sb, wk_sb)[k // 2]
                    for c in range(NC):
                        mm = eng.matmul(bank[:, :], w[:, c, k % 2, :], xnT[:, c, bass.ds((b + 2) * T, T)],
                                        start=(c == 0), stop=(c == NC - 1))
                    return mm

                def project_v(i):
                    bank = shared["v", i]
                    if i == 0:
                        eng.wait_ge(xnv_in, 16 * (b + 1))
                    for t in range(2):
                        for c in range(NC):
                            mm = eng.matmul(bank[:, t * D:(t + 1) * D],
                                            xn_v[:, c, (2 * i + t) * P:(2 * i + t + 1) * P],
                                            wv_sb[:, c, :], start=(c == 0), stop=(c == NC - 1))
                    return mm

                def turn_heads(qb):
                    bank = shared["o", qb]
                    eng.wait_ge(heads_copied, 4 * b)
                    for g in range(NG):
                        mm = eng.transpose(bank[:, g * P:(g + 1) * P], heads[:, g, qb * P:(qb + 1) * P],
                                           ident[:, :])
                    return mm

                def turn_attn(qb):
                    bank = shared["at", qb]
                    eng.wait_ge(normed, 4 * (b - 1) + qb + 1)
                    for c in range(NC):
                        mm = eng.transpose(bank[:, c * P:(c + 1) * P], attn[:, qb, c * P:(c + 1) * P],
                                           ident[:, :])
                    return mm

                def outputs(qb):
                    bank = shared["fin", qb]
                    eng.wait_ge(at_copied, 4 * (b - 1) + qb + 1)
                    for c in range(NC):
                        eng.matmul(bank[:, 0:D], attnT[:, qb % 2, c, :], wo_sb[:, c, :],
                                   start=(c == 0), stop=False)
                    if qb == 0:
                        eng.wait_ge(xq_done, b)
                    for c in range(NC):
                        mm = eng.matmul(bank[:, 0:D], xq[:, c, qb * P:(qb + 1) * P], wf_q[:, c, :],
                                        start=False, stop=(c == NC - 1))
                    return mm

                def turn_max(i):
                    bank = shared["mt", i]
                    eng.wait_ge(max_done, ITEMS * (b + ahead["mt"][i]) + ITEMS // 2 * (i + 1))
                    return eng.transpose(bank[0:H * NQ // 2, 0:P],
                                         rowmax[:, H * NQ // 2 * i:H * NQ // 2 * (i + 1)], ident[:, :])

                def pv(bb, g, step):
                    for kb in ((0,), (1, 3), (2,))[step]:
                        if kb == 0:
                            wait_past(eng, heads_copied, 4 * bb + g)
                        if g == 0 and kb < 2:
                            eng.wait_ge(v_copied, 2 * bb + kb + 1)
                        eng.wait_ge(masked, SLOTS * bb + 5 * g + (2, 4, 5)[step])
                        for u in ((0, 1), (2, 3), (4,))[step]:
                            for i, k, col in [(i, k, T * half + col) for half in range(2)
                                              for i, k, col in unit_parts(u, half)]:
                                if k == kb:
                                    mm = eng.matmul(o_ps[32 * i:32 * i + 2 * DH, kb * P:T],
                                                    v_sb[:, kb, g * HG + i, :],
                                                    prob[u][:, col:col + T - kb * P],
                                                    start=(kb == 0), stop=(kb == 2),
                                                    skip_group_check=True)
                    mm.then_inc(pv_done, 1)

                todo = work(stages)
                done_before = work(before)

                def bank_free(at):
                    bank = SHARED_BANK[todo[at][1:]]
                    past = [(b, m) for m in todo[:at] if SHARED_BANK[m[1:]] == bank] or \
                           [(b - 1, m) for m in done_before if SHARED_BANK[m[1:]] == bank]
                    if past:
                        b_, (_, kind, k) = past[-1]
                        done, per = reader[kind]
                        eng.wait_ge(done, per * (b_ + ahead[kind][k]) + k + 1)

                do = {"qk": project, "v": project_v, "o": turn_heads, "at": turn_attn, "fin": outputs,
                      "mt": turn_max}
                for s in range(SLOTS):
                    if 3 in stages:
                        scores(s)
                    elif 2 in stages:
                        scores_for_max(2 * s)
                    for at, item in enumerate(todo):
                        if item[0] != s:
                            continue
                        bank_free(at)
                        do[item[1]](item[2]).then_inc(full[item[1]], 1)
                    if 2 in stages:
                        scores_for_max(2 * s + 1)
                    if 4 in stages and s < 2:
                        pv(b - 1, NG - 1, s + 1)
                    if 3 in stages:
                        for lag, step in ((3, 0), (5, 1), (6, 2)):
                            if s >= lag and (s - lag) % 5 == 0 and (s - lag) // 5 < NG:
                                pv(b, (s - lag) // 5, step)

            run(eng, iteration)


def kernel(L0_attn_X, L0_attn_W_q, L0_attn_W_k, L0_attn_W_v, L0_attn_W_o, L0_ffn_weight, L0_ffn_bias):
    import concourse.bacc as bacc
    from concourse.bass_utils import run_bass_kernel_spmd

    def turned(w):
        return np.ascontiguousarray(np.asarray(w).T)

    def pairs(w):
        return np.ascontiguousarray(np.asarray(w).reshape(H, J, 2, D).transpose(3, 2, 1, 0).reshape(D, 2, J * H))

    theta = (np.float32(10000.0) ** (np.float32(-2.0) * np.arange(J, dtype=np.float32) / np.float32(DH)))
    angles = (np.arange(T, dtype=np.float32)[:, None] * theta.astype(np.float32)[None, :]).T
    cos = np.ascontiguousarray(np.repeat(np.cos(angles), H, axis=0).astype(np.float32))
    sin = np.ascontiguousarray(np.repeat(np.sin(angles), H, axis=0).astype(np.float32))

    arrays = {"x": np.ascontiguousarray(np.asarray(L0_attn_X)), "wq": pairs(L0_attn_W_q), "wk": pairs(L0_attn_W_k),
              "wv": turned(L0_attn_W_v), "wo": turned(L0_attn_W_o), "wf": turned(L0_ffn_weight),
              "bias": np.ascontiguousarray(np.asarray(L0_ffn_bias)), "cos": cos, "sin": sin}
    nc = bacc.Bacc("TRN2", target_bir_lowering=False, num_devices=1)
    args = [nc.dram_tensor(f"{k}_dram", a.shape, F32, kind="ExternalInput").ap() for k, a in arrays.items()]
    args.append(nc.dram_tensor("out_dram", (NB, T, D), F32, kind="ExternalOutput").ap())
    attention_ffn_block(nc, *args)
    r = run_bass_kernel_spmd(nc, [{f"{k}_dram": a for k, a in arrays.items()}], core_ids=[0])
    return r.results[0]["out_dram"]
```

```python
from contextlib import ExitStack

import numpy as np

import concourse.bass as bass
from concourse import mybir

F32 = mybir.dt.float32
BF16 = mybir.dt.bfloat16
F32R = mybir.dt.float32r
U32 = mybir.dt.uint32
ALU = mybir.AluOpType
ACT = mybir.ActivationFunctionType
AX = mybir.AxisListType

P = 128
NB, T, D = 8, 512, 256
H, DH = 16, 16
J = DH // 2
NQ = T // P
NC = D // P
HG = 4
NG = H // HG
SLOTS = 5 * NG
PAIR = 2 * T
SCALE = float(DH) ** -0.5
EPS = 1e-5
FP8_MAX = 448.0
NEG = -3.0e38
Q_PARTS = ((0, 1), (0, 1, 2), (0,))
K_PARTS = ((0, 1, 2), (0,), (0, 1))
ROWS = 6 * DH
VW = DH + 1
SHIFT = 2

MAX_BANKS = [[(0, 3, 0)], [(0, 0, 0), (0, 2, P)], [(1, 3, 0)], [(1, 0, 0), (1, 2, P)], [(0, 1, 0), (1, 1, 2 * P)]]
BANKS = H // 2 * len(MAX_BANKS)
ITEMS = H * NQ
ITEMS_UP_TO = [sum(len(MAX_BANKS[i % len(MAX_BANKS)]) for i in range(f + 1)) for f in range(BANKS)]
assert BANKS == 2 * SLOTS and ITEMS_UP_TO[-1] == ITEMS

MISC = [(0, "mt", 1), (0, "v", 0), (1, "qk", 0), (2, "qk", 1), (3, "v", 1), (4, "qk", 2), (5, "o", 0),
        (6, "o", 1), (6, "qk", 3), (7, "o", 2), (8, "o", 3), (9, "at", 0), (10, "at", 1), (11, "mt", 0),
        (12, "fin", 0), (13, "at", 2), (14, "fin", 1), (15, "at", 3), (17, "fin", 2), (19, "fin", 3)]
SHARED_BANK = {(kind, k): i % 2 for i, (_, kind, k) in enumerate(MISC)}


HALVES = 2 * SLOTS
ST_BANK = [i % 3 for i in range(HALVES - 1)] + [1]
ST_BEFORE = [max(j for j in range(-HALVES, i) if ST_BANK[j % HALVES] == ST_BANK[i]) for i in range(HALVES)]


def wait_past(eng, sem, count):
    if not (isinstance(count, int) and count <= 0):
        eng.wait_ge(sem, count)


def each_batch(eng, step, between):
    for n in range(4):
        step(n, n % 2)
        between(n)
    with eng.Fori(2, NB // 2) as i:
        for p in range(2):
            step(2 * i + p, p)


def unit_parts(u, half):
    if u < 2:
        return [(2 * u + half, 0, 0)]
    if u < 4:
        return [(2 * (u - 2) + half, 3, 0), (2 * (u - 2) + half, 1, P)]
    return [(2 * half + i, 2, 2 * P * i) for i in range(2)]


def attention_ffn_block(nc, x, wq, wk, wv, wo, wf, bias, cos, sin, out):
    with ExitStack() as ctx:
        def sb(name, shape, dt=F32):
            return ctx.enter_context(nc.sbuf_tensor(name, shape, dt))

        def pb(name, shape):
            return ctx.enter_context(nc.psum_tensor(name, shape, F32))

        def sem(name):
            return ctx.enter_context(nc.semaphore(name))

        w_parts = [sb(f"{name}_parts", [P, 2, NC, 2, P], F32R) for name in ("wq", "wk")]
        wv_sb = sb("wv_sb", [P, NC, D])
        wo_sb = sb("wo_sb", [P, NC, D])
        wf_q = sb("wf_q", [P, NC, D], BF16)
        bias_sb = sb("bias_sb", [P, D])
        cos_sb = sb("cos_sb", [P, T])
        sin_sb = sb("sin_sb", [P, T])
        ident = sb("ident", [P, P])
        ones2 = sb("ones2", [2, P])
        causal = sb("causal", [P, T], BF16)
        xnT = sb("xnT", [P, NC, NB * T])
        xn_v = sb("xn_v", [P, NC, T])
        q_st = sb("q_st", [P, 2, H, T], BF16)
        k_st = sb("k_st", [P, 2, H, T], BF16)
        v_sb = sb("v_sb", [P, NQ, H, VW])
        prob = [sb(f"prob{u}", [P, PAIR]) for u in range(5)]
        heads = sb("heads", [P, NG, T])
        prod = sb("prod", [P, 4, T])
        rot = sb("rot", [P, 2, T])
        x_parts = sb("x_parts", [P, 2, NC, T], F32R)
        parts = sb("parts", [P, 2, 3, 2, T], BF16)
        scratch = sb("scratch", [P, 2, T], BF16)
        rowmax = sb("rowmax", [P, H * NQ])
        shift = sb("shift", [H * NQ // 2, SHIFT, P], BF16)
        rden = sb("rden", [P, H])
        attn = sb("attn", [P, NQ, D])
        attnT = sb("attnT", [P, 2, NC, P])
        x_res = sb("x_res", [P, NQ, D])
        xq = sb("xq", [P, NC, T], BF16)
        stats = sb("stats", [P, 2, NQ, 6])
        mv_b = sb("mv_b", [P, 2, NQ, 2])
        ve = sb("ve", [P, 2, NQ])
        nmean = sb("nmean", [P, 2, NQ])
        half = sb("half", [P, NQ])
        rstd = sb("rstd", [P, 2, NQ])
        shift_x = sb("shift_x", [P, 2, NQ])
        amax = sb("amax", [P, NB + 1])
        amax2 = sb("amax2", [P, 2])
        amax_r = sb("amax_r", [2, 1])
        amax_d = sb("amax_d", [2, 2])
        amax_b = sb("amax_b", [P, 2])
        inv = sb("inv", [P, 2])
        scale = sb("scale", [P, 2])
        unscale = sb("unscale", [P, 2])
        both = sb("both", [P, 1])
        x_all = q_st[:, :, :, :].rearrange("p a h t -> p (a h t)").bitcast(F32).rearrange(
            "p (b n d) -> p b n d", b=NB, n=NQ)
        xn = [prob[i][:, :].rearrange("p (n d) -> p n d", n=NQ) for i in range(2)]
        wq_sb, wk_sb = [prob[2][:, i * NC * D:(i + 1) * NC * D].rearrange("p (c r m) -> p c r m", c=NC, r=2)
                        for i in range(2)]
        wf_sb = prob[3][:, 0:NC * D].rearrange("p (c n) -> p c n", c=NC)
        qv = sb("qv", [P, NC * T])
        qe = sb("qe", [P, NC * T])

        st_ps = [pb(f"st_ps{i}", [P, T]) for i in range(3)]
        s_ps = [pb(f"s_ps{i}", [P, T]) for i in range(2)]
        o_ps = pb("o_ps", [P, T])
        m_ps = [pb(f"m_ps{i}", [P, T]) for i in range(2)]
        shared = {(kind, k): m_ps[bank] for (kind, k), bank in SHARED_BANK.items()}

        turn_ps = [[st_ps[0], st_ps[1]], [st_ps[2], o_ps]]

        first_ps = m_ps + s_ps

        qk_dram = nc.dram_tensor("qk_parts", [2, 2, 3, 2, J, H, T], BF16, kind="Internal").ap()
        shift_dram = nc.dram_tensor("shift_rows", [2, SHIFT, H * NQ // 2, P], BF16, kind="Internal").ap()

        w_qk_in = sem("w_qk_in")
        w_in = sem("w_in")
        x_in = [sem(f"x_in{i}") for i in range(2)]
        xnv_in = sem("xnv_in")
        res_in = sem("res_in")
        parts_out = sem("parts_out")
        stack_in = [sem(f"stack_in{g}") for g in range(NG)]
        shift_out = [sem(f"shift_out{i}") for i in range(2)]
        shift_in = [sem(f"shift_in{i}") for i in range(2)]
        y_out = sem("y_out")
        consts = sem("consts")
        ln_stat = sem("ln_stat")
        ln_agg = sem("ln_agg")
        ln_ve = sem("ln_ve")
        ln_rstd = sem("ln_rstd")
        xn_done = sem("xn_done")
        xn_turned = sem("xn_turned")
        xnT_copied = sem("xnT_copied")
        amax_done = sem("amax_done")
        amax_turned = sem("amax_turned")
        wquant = sem("wquant")
        wf_scaled = sem("wf_scaled")
        qw_exp = sem("qw_exp")
        w_high = sem("w_high")
        w_split = sem("w_split")
        x_high = sem("x_high")
        x_split = sem("x_split")
        wo_scaled = sem("wo_scaled")
        st_full = sem("st_full")
        s_full = sem("s_full")
        full = {k: sem(f"{k}_full") for k in ("qk", "v", "o", "at", "fin", "mt")}
        pv_done = sem("pv_done")
        exp_done = sem("exp_done")
        max_done = sem("max_done")
        roped = sem("roped")
        v_copied = sem("v_copied")
        heads_copied = sem("heads_copied")
        recip_done = sem("recip_done")
        normed = sem("normed")
        at_copied = sem("at_copied")
        fin_done = sem("fin_done")
        shift_hi = sem("shift_hi")
        shift_done = sem("shift_done")
        masked = sem("masked")
        max_begun = sem("max_begun")
        mask_begun = sem("mask_begun")
        agg_begun = sem("agg_begun")
        rotated = sem("rotated")
        hi_done = sem("hi_done")
        rem_done = sem("rem_done")
        mid_done = sem("mid_done")
        low_done = sem("low_done")
        qv_done = sem("qv_done")
        qe_done = sem("qe_done")
        qc_done = sem("qc_done")
        qw_done = sem("qw_done")
        xq_done = sem("xq_done")
        res_done = sem("res_done")

        reader = {"qk": (roped, 4), "v": (v_copied, 2), "o": (normed, 4), "at": (at_copied, 4),
                  "fin": (fin_done, 4), "mt": (shift_done, 2)}
        ahead = {"qk": (2,) * 4, "v": (0,) * 2, "o": (-1,) * 4, "at": (-1,) * 4, "fin": (-1,) * 4, "mt": (1, 0)}

        def work(stages):
            stage_of = {2: 1, 1: 2, 0: 3, -1: 4}
            return [(s, kind, k) for s, kind, k in MISC if stage_of[ahead[kind][k]] in stages]

        def rotated_in(n, w):
            own = isinstance(n, int) and (n, w) == (0, 1)
            return heads[:, 0:2, :] if own else rot[:, :, :]

        def rotate(eng, n, w):
            eng.wait_ge(roped, 4 * n + 2 * w + 2)
            if not (isinstance(n, int) and n == 0):
                eng.wait_ge(low_done, 2 * n + w)
            dst = rotated_in(n, w)
            eng.tensor_tensor(dst[:, 0, :], prod[:, 0, :], prod[:, 2, :], ALU.subtract).then_inc(rotated, 1)
            eng.tensor_tensor(dst[:, 1, :], prod[:, 1, :], prod[:, 3, :], ALU.add).then_inc(rotated, 1)

        def remainder(eng, n, w):
            eng.wait_ge(rotated, 4 * n + 2 * w + 2)
            eng.wait_ge(hi_done, 2 * n + w + 1)
            buf = rotated_in(n, w)
            eng.tensor_tensor(buf, buf, parts[:, w, 0], ALU.subtract).then_inc(rem_done, 1)

        def low(eng, n, w):
            eng.wait_ge(mid_done, 2 * n + w + 1)
            eng.tensor_tensor(parts[:, w, 2], rotated_in(n, w), parts[:, w, 1], ALU.subtract).then_inc(low_done, 1)

        block = ctx.enter_context(nc.Block())

        LOOP = (2, 6)

        def run(eng, iteration):
            every = {1, 2, 3, 4}
            iteration(-1, 1, {2}, set())
            iteration(0, 0, {1, 2, 3}, {1, 2})
            iteration(1, 1, every, {1, 2, 3})
            with eng.Fori(0, (LOOP[1] - LOOP[0]) // 2) as i:
                iteration(2 * i + LOOP[0], 0, every, every)
                iteration(2 * i + LOOP[0] + 1, 1, every, every)
            iteration(6, 0, {2, 3, 4}, every)
            iteration(7, 1, {3, 4}, {2, 3, 4})
            iteration(8, 0, {4}, {3, 4})

        @block.sync
        def _(eng):
            def load_x(n, p):
                wait_past(eng, x_in[p], 8 * (n - p))
                eng.dma_start(x_all[:, bass.ds(n, 1)].rearrange("p a n d -> p (a n) d"),
                              x[bass.ds(n, 1)].rearrange("a (n p) d -> p (a n) d", p=P)).then_inc(x_in[p], 16)

            def load_weights(n):
                if n == 0:
                    for dst, src in ((wq_sb, wq), (wk_sb, wk)):
                        eng.dma_start(dst, src.rearrange("(c p) r m -> p c r m", p=P))\
                           .then_inc(w_qk_in, 16)
                    eng.dma_start(cos_sb[:, :], cos).then_inc(w_qk_in, 16)
                    eng.dma_start(sin_sb[:, :], sin).then_inc(w_qk_in, 16)
                elif n == 3:
                    for dst, src in ((wf_sb, wf), (wv_sb[:, :, :], wv), (wo_sb[:, :, :], wo)):
                        eng.dma_start(dst, src.rearrange("(c p) n -> p c n", p=P)).then_inc(w_in, 16)
                    eng.dma_start(bias_sb[:, :], bias.partition_broadcast(P)).then_inc(w_in, 16)

            each_batch(eng, load_x, load_weights)
            def iteration(b, par, stages, before):
                if 3 in stages:
                    shift_rows(b, par, 1)
                if 4 in stages:
                    wait_past(eng, y_out, 16 * (b - 1))
                    eng.dma_start(x_res[:, :, :], x[bass.ds(b - 1, 1)].rearrange("a (n p) d -> p (a n) d", p=P))\
                       .then_inc(res_in, 16)
                if 3 in stages and 2 in stages:
                    eng.wait_ge(full["v"], 2 * (b + 1))
                    eng.dma_start(xn_v[:, :, :], xnT[:, :, bass.ds((b + 1) * T, T)]).then_inc(xnv_in, 16)
                if 1 in stages:
                    query_stacks(b + 2, par, 3 in stages)
                if 2 in stages:
                    shift_rows(b + 1, 1 - par, 0)
                if 1 in stages:
                    key_stacks(b + 2, par, 3 in stages)
                if 4 in stages:
                    eng.wait_ge(fin_done, 4 * b)
                    eng.dma_start(out[bass.ds(b - 1, 1)].rearrange("a (n p) d -> p (a n) d", p=P),
                                  x_res[:, :, :]).then_inc(y_out, 16)

            def qk_view(par, which):
                return qk_dram[par, which].rearrange("t r j h n -> (j h) (t r) n")

            def query_stacks(n, par, busy):
                eng.wait_ge(low_done, 2 * n + 1)
                eng.dma_start(qk_view(par, 0),
                              parts[:, 0].rearrange("p t r n -> p (t r) n")).then_inc(parts_out, 16)
                eng.wait_ge(parts_out, 32 * n + 16)
                if isinstance(n, int) and n < 2:
                    eng.wait_ge(xn_done, NB // 2 * NQ * (n + 1))
                for g in range(2):
                    read_stack(n, par, g, "q", busy)

            def key_stacks(n, par, busy):
                eng.wait_ge(low_done, 2 * n + 2)
                eng.dma_start(qk_view(par, 1),
                              parts[:, 1].rearrange("p t r n -> p (t r) n")).then_inc(parts_out, 16)
                eng.wait_ge(parts_out, 32 * n + 32)
                for g in range(NG):
                    read_stack(n, par, g, "k", busy)
                    if g >= 2:
                        read_stack(n, par, g, "q", False)

            def read_stack(n, par, g, which, busy):
                if busy:
                    eng.wait_ge(st_full, HALVES * (n - 2) + 10 * (g + 1))
                h0 = g * HG
                dst, runs, w = (q_st, Q_PARTS, 0) if which == "q" else (k_st, K_PARTS, 1)
                src = qk_dram[par, w].rearrange("t r j h n -> (t r j) h n")
                row = 0
                for run_ in runs:
                    rows = DH * len(run_)
                    eng.dma_start(dst[row:row + rows, par, h0:h0 + HG, :],
                                  src[DH * run_[0]:DH * run_[0] + rows, h0:h0 + HG, :]).then_inc(stack_in[g], 16)
                    row += rows

            def shift_rows(n, par, half_):
                eng.wait_ge(shift_done, 2 * n + half_ + 1)
                eng.dma_start(shift_dram[half_].rearrange("t a n -> a t n"), shift[:, :, :])\
                   .then_inc(shift_out[half_], 16)
                eng.wait_ge(shift_out[half_], 16 * (n + 1))
                h0 = half_ * (H // 2)
                eng.dma_start(q_st[ROWS:ROWS + SHIFT, par, h0:h0 + H // 2, :],
                              shift_dram[half_].rearrange("t a n -> t (a n)").rearrange(
                                  "t (h n) -> t h n", h=H // 2)).then_inc(shift_in[half_], 16)

            query_stacks(0, 0, False)
            key_stacks(0, 0, False)
            query_stacks(1, 1, False)
            key_stacks(1, 1, False)
            eng.wait_ge(xnT_copied, 2 * NB)
            eng.dma_start(xn_v[:, :, :], xnT[:, :, 0:T]).then_inc(xnv_in, 16)
            run(eng, iteration)
            eng.wait_ge(y_out, 16 * NB)

        @block.gpsimd
        def _(eng):
            eng.memset(ident[:, :], 0.0).then_inc(consts, 1)
            eng.memset(half[:, :], -0.5).then_inc(consts, 1)
            eng.memset(causal[:, :], 0.0).then_inc(consts, 1)
            eng.memset(ones2[:, :], 1.0).then_inc(consts, 1)
            eng.wait_ge(consts, 4)
            eng.affine_select(out=ident[:, :], in_=ident[:, :], compare_op=ALU.not_equal, fill=1.0,
                              base=0, pattern=[[-1, P]], channel_multiplier=1).then_inc(consts, 1)
            eng.affine_select(out=causal[:, T - P:T], in_=causal[:, T - P:T], compare_op=ALU.is_ge, fill=NEG,
                              base=0, pattern=[[-1, P]], channel_multiplier=1).then_inc(consts, 1)

            def invert(n, p):
                eng.wait_ge(ln_ve, 2 * n + 2)
                wait_past(eng, xn_done, NQ * (n - 1))
                eng.tensor_tensor(rstd[:, p, :], ve[:, p, :], half[:, :], ALU.pow).then_inc(ln_rstd, 1)
                eng.wait_ge(ln_rstd, 2 * n + 1)
                eng.tensor_tensor(shift_x[:, p, :], nmean[:, p, :], rstd[:, p, :], ALU.mult).then_inc(ln_rstd, 1)

            def rotate_second(n):
                if n == 3:
                    rotate(eng, 1, 0)

            each_batch(eng, invert, rotate_second)
            remainder(eng, 1, 0)
            low(eng, 1, 0)
            rotate(eng, 1, 1)
            remainder(eng, 1, 1)
            low(eng, 1, 1)
            def iteration(b, par, stages, before):
                n = b + 2

                def mask(s):
                    u = s % 5
                    if u < 2:
                        ap, pat = prob[u].rearrange("p (h q) -> p h q", h=2)[:, :, 0:P], [[0, 2], [1, P]]
                    elif u < 4:
                        ap = prob[u].rearrange("p (h q) -> p h q", h=2)[:, :, 0:2 * P]
                        pat = [[0, 2], [0, 2], [1, P]]
                    else:
                        ap, pat = prob[u].rearrange("p (h q) -> p h q", h=4)[:, :, 0:P], [[0, 4], [1, P]]
                    eng.wait_ge(exp_done, HALVES * b + 2 * (s + 1))
                    eng.sem_inc(mask_begun)
                    eng.affine_select(out=ap, in_=ap, compare_op=ALU.is_ge, fill=0.0, base=0,
                                      pattern=pat, channel_multiplier=-1).then_inc(masked, 1)

                for s in range(SLOTS):
                    if 1 in stages and s == 0:
                        eng.wait_ge(x_high, n - 1)
                        eng.tensor_tensor(x_parts[:, 1], xnT[:, :, bass.ds(n * T, T)],
                                          x_parts[:, 0].bitcast(F32), ALU.subtract).then_inc(x_split, 1)
                    if 3 in stages:
                        mask(s)
                    if 1 in stages:
                        if s in (7, 13):
                            low(eng, n, s // 13)
                        if s in (3, 8):
                            rotate(eng, n, s // 8)
                        if s in (5, 10):
                            remainder(eng, n, s // 10)
                    if 4 in stages:
                        if s == 9:
                            eng.wait_ge(res_in, 16 * b)
                            eng.tensor_tensor(x_res[:, :, :], x_res[:, :, :],
                                              bias_sb[:, None, :].to_broadcast([P, NQ, D]), ALU.add)\
                               .then_inc(res_done, 1)
                        if s == 4:
                            eng.wait_ge(qc_done, b)
                            eng.tensor_tensor(qv[:, :], qv[:, :], qe[:, :], ALU.add).then_inc(qw_done, 1)
                        if s == 6:
                            eng.wait_ge(qw_done, b)
                            wait_past(eng, full["fin"], 4 * (b - 1))
                            eng.tensor_tensor(xq.rearrange("p c t -> p (c t)"), qv[:, :], qe[:, :],
                                              ALU.subtract).then_inc(xq_done, 1)

            for w, (parts_of, raw) in enumerate(zip(w_parts, (wq_sb, wk_sb))):
                eng.wait_ge(w_high, w + 1)
                eng.tensor_tensor(parts_of[:, 1], raw, parts_of[:, 0].bitcast(F32), ALU.subtract).then_inc(w_split, 1)
            nw = NC * D
            eng.wait_ge(wquant, 8)
            eng.tensor_tensor(qv[:, 0:nw], qv[:, 0:nw], qe[:, 0:nw], ALU.add).then_inc(wquant, 1)
            eng.wait_ge(wquant, 9)
            eng.tensor_tensor(wf_q[:, :, :].rearrange("p c n -> p (c n)"), qv[:, 0:nw], qe[:, 0:nw],
                              ALU.subtract).then_inc(wquant, 1)
            eng.memset(v_sb[:, :, :, :], 1.0).then_inc(consts, 1)
            eng.wait_ge(consts, 7)
            eng.memset(k_st[ROWS:ROWS + SHIFT, :, :, :].rearrange("p a h t -> p (a h t)").bitcast(F32),
                       float(np.array([0x3F803F80], np.uint32).view(np.float32)[0])).then_inc(consts, 1)
            eng.wait_ge(consts, 8)
            eng.wait_ge(w_in, 16 * 4)
            run(eng, iteration)

        @block.vector
        def _(eng):
            def statistics(n, p):
                eng.wait_ge(x_in[p], 8 * (n - p) + 16)
                for t in range(NQ):
                    eng.bn_stats(stats[:, p, t, :], x_all[:, bass.ds(n, 1), t, :].rearrange("p a d -> p (a d)"))\
                       .then_inc(ln_stat, 1)
                if not (isinstance(n, int) and n < 2):
                    largest(n - 2, p)
                eng.wait_ge(ln_stat, NQ * (n + 1))
                eng.sem_inc(agg_begun)
                for t in range(NQ):
                    eng.bn_aggr(mv_b[:, p, t, :], stats[:, p, t, :]).then_inc(ln_agg, 1)
                eng.wait_ge(ln_agg, NQ * (n + 1))
                wait_past(eng, ln_rstd, 2 * (n - 1))
                eng.tensor_scalar(ve[:, p, :], mv_b[:, p, :, 1], EPS, None, ALU.add).then_inc(ln_ve, 1)
                eng.tensor_scalar(nmean[:, p, :], mv_b[:, p, :, 0], -1.0, None, ALU.mult).then_inc(ln_ve, 1)

            def largest(n, p):
                eng.wait_ge(xn_done, NQ * (n + 1))
                eng.tensor_reduce(amax[:, bass.ds(n, 1)], xn[p], AX.XY, ALU.max,
                                  apply_absolute_value=True).then_inc(amax_done, 1)

            def rope(n, k, bank):
                r = k % 2
                eng.wait_ge(full["qk"], 4 * n + k + 1)
                if r == 0:
                    wait_past(eng, rotated, 4 * n + k)
                a, c = (prod[:, 0, :], prod[:, 1, :]) if r == 0 else (prod[:, 3, :], prod[:, 2, :])
                eng.tensor_tensor(a, bank[:, :], cos_sb[:, :], ALU.mult)
                eng.tensor_tensor(c, bank[:, :], sin_sb[:, :], ALU.mult).then_inc(roped, 1)

            def rope_first(n):
                if n == 3:
                    eng.wait_ge(w_qk_in, 16 * 4)
                    rope(0, 0, first_ps[0])
                    rope(0, 1, first_ps[1])
                    rotate(eng, 0, 0)
                    rope(0, 2, first_ps[2])
                    rope(0, 3, first_ps[3])
                    remainder(eng, 0, 0)
                    rotate(eng, 0, 1)
                    low(eng, 0, 0)
                    remainder(eng, 0, 1)
                    low(eng, 0, 1)
                    rope(1, 0, first_ps[0])
                    rope(1, 1, first_ps[1])

            each_batch(eng, statistics, rope_first)
            rope(1, 2, first_ps[2])
            rope(1, 3, first_ps[3])
            largest(NB - 2, 0)
            largest(NB - 1, 1)
            def weight_step(s):
                nw = NC * D
                if s == 1:
                    eng.wait_ge(w_in, 16 * 4)
                    eng.tensor_reduce(amax[:, NB:NB + 1], wf_sb[:, :, :], AX.XY, ALU.max,
                                      apply_absolute_value=True).then_inc(amax_done, 1)
                    eng.wait_ge(amax_done, NB + 1)
                    eng.tensor_reduce(amax2[:, 0:1], amax[:, 0:NB], AX.X, ALU.max).then_inc(amax_done, 1)
                    eng.tensor_copy(amax2[:, 1:2], amax[:, NB:NB + 1]).then_inc(amax_done, 1)
                if s == 3:
                    eng.wait_ge(amax_turned, 1)
                    eng.tensor_reduce(amax_r[:, :], o_ps[0:2, 0:P], AX.X, ALU.max).then_inc(wquant, 1)
                    eng.wait_ge(consts, 6)
                    eng.wait_ge(wquant, 1)
                    eng.tensor_scalar(amax_d[:, :], ident[0:2, 0:2], amax_r[:, 0:1], None, ALU.mult)\
                       .then_inc(wquant, 1)
                if s == 5:
                    eng.wait_ge(amax_turned, 2)
                    eng.tensor_scalar(amax_b[:, :], o_ps[:, 0:2], 1e-12, None, ALU.max).then_inc(wquant, 1)
                    eng.wait_ge(wquant, 3)
                    eng.reciprocal(inv[:, :], amax_b[:, :]).then_inc(wquant, 1)
                    eng.tensor_scalar(unscale[:, :], amax_b[:, :], 1.0 / FP8_MAX, None, ALU.mult).then_inc(wquant, 1)
                    eng.wait_ge(wquant, 5)
                    eng.tensor_scalar(scale[:, :], inv[:, :], FP8_MAX, None, ALU.mult).then_inc(wquant, 1)
                    eng.tensor_tensor(both[:, :], unscale[:, 0:1], unscale[:, 1:2], ALU.mult).then_inc(wquant, 1)
                if s == 7:
                    eng.wait_ge(wf_scaled, 1)
                    eng.tensor_scalar(qe[:, 0:nw].bitcast(U32), qv[:, 0:nw].bitcast(U32), 0x7F800000, None,
                                      ALU.bitwise_and).then_inc(qw_exp, 1)
                if s == 8:
                    eng.wait_ge(qw_exp, 1)
                    eng.tensor_scalar(qe[:, 0:nw], qe[:, 0:nw], 2.0 ** -6, 1.5 * 2.0 ** 20, ALU.max, ALU.mult)\
                       .then_inc(wquant, 1)

            def iteration(b, par, stages, before):
                def row_max(f):
                    pair, m = divmod(f, len(MAX_BANKS))
                    eng.wait_ge(s_full, BANKS * (b + 1) + f + 1)
                    if f == 0:
                        wait_past(eng, full["mt"], 2 * b + 1)
                    if f == BANKS // 2:
                        wait_past(eng, full["mt"], 2 * b + 2)
                    eng.sem_inc(max_begun)
                    for h, qb, col in MAX_BANKS[m]:
                        e = (2 * pair + h) * NQ + qb
                        w = P * (qb + 1)
                        eng.tensor_tensor_reduce(scratch[:, f % 2, col:col + w], s_ps[f % 2][:, col:col + w],
                                                 causal[:, T - w:T], 1.0, NEG, ALU.add, ALU.max,
                                                 rowmax[:, e:e + 1]).then_inc(max_done, 1)

                def norm(qb):
                    bank = shared["o", qb]
                    o = bank[:, :].rearrange("p (h w) -> p h w", h=H)
                    eng.wait_ge(full["o"], 4 * (b - 1) + qb + 1)
                    wait_past(eng, normed, 4 * (b - 1) + qb)
                    eng.reciprocal(rden[:, :, None], o[:, :, DH:DH + 1]).then_inc(recip_done, 1)
                    eng.wait_ge(recip_done, 4 * (b - 1) + qb + 1)
                    if qb == 0:
                        wait_past(eng, full["at"], 4 * (b - 1))
                    eng.tensor_tensor(attn[:, qb, :].rearrange("p (h w) -> p h w", h=H), o[:, :, 0:DH],
                                      rden[:, :, None].to_broadcast([P, H, DH]), ALU.mult).then_inc(normed, 1)

                def finish(qb):
                    bank = shared["fin", qb]
                    eng.wait_ge(full["fin"], 4 * (b - 1) + qb + 1)
                    if qb == 0:
                        eng.wait_ge(res_done, b)
                    eng.scalar_tensor_tensor(out=x_res[:, qb, :], in0=bank[:, 0:D], scalar=both[:, 0:1],
                                             in1=x_res[:, qb, :], op0=ALU.mult, op1=ALU.add)\
                       .then_inc(fin_done, 1)

                def split_max(i):
                    bank = shared["mt", i]
                    n = b + ahead["mt"][i]
                    c = 2 * n + i
                    rows = H * NQ // 2
                    eng.wait_ge(full["mt"], c + 1)
                    wait_past(eng, shift_out[1 - i], 16 * (n + i))
                    eng.tensor_scalar(shift[:, 0, :], bank[0:rows, 0:P], -1.0, None, ALU.mult).then_inc(shift_hi, 1)
                    eng.wait_ge(shift_hi, c + 1)
                    eng.scalar_tensor_tensor(out=shift[:, 1, :], in0=bank[0:rows, 0:P], scalar=-1.0,
                                             in1=shift[:, 0, :], op0=ALU.mult, op1=ALU.subtract)\
                       .then_inc(shift_done, 1)

                for s in range(SLOTS):
                    if 2 in stages:
                        row_max(2 * s)
                        row_max(2 * s + 1)
                        if 3 not in stages:
                            weight_step(s)
                    for slot, kind, k in work(stages):
                        if slot == s and kind in ("qk", "o", "fin", "mt"):
                            {"qk": lambda i: rope(b + 2, i, shared["qk", i]), "o": norm, "fin": finish, "mt": split_max}[kind](k)
                    if s == 1 and 4 in stages:
                        eng.wait_ge(qv_done, b)
                        eng.tensor_scalar(qe[:, :].bitcast(U32), qv[:, :].bitcast(U32), 0x7F800000, None,
                                          ALU.bitwise_and).then_inc(qe_done, 1)
                    if s == 3 and 4 in stages:
                        eng.wait_ge(qe_done, b)
                        eng.tensor_scalar(qe[:, :], qe[:, :], 2.0 ** -6, 1.5 * 2.0 ** 20, ALU.max, ALU.mult)\
                           .then_inc(qc_done, 1)

            run(eng, iteration)

        @block.scalar
        def _(eng):
            def normalise(n, p):
                eng.wait_ge(ln_rstd, 2 * n + 2)
                wait_past(eng, amax_done, n - 1)
                wait_past(eng, xn_turned, 2 * n - 2)
                for t in range(NQ):
                    eng.activation(xn[p][:, t, :], x_all[:, bass.ds(n, 1), t, :].rearrange("p a d -> p (a d)"),
                                   ACT.Identity, bias=shift_x[:, p, t:t + 1], scale=rstd[:, p, t:t + 1])\
                       .then_inc(xn_done, 1)
                if not (isinstance(n, int) and n == 0):
                    copy_turned(n - 1, 1 - p)

            def copy_turned(n, p):
                for c in range(NC):
                    eng.wait_ge(xn_turned, 2 * n + c + 1)
                    eng.copy(xnT[:, c, bass.ds(n * T, T)], turn_ps[p][c][:, :]).then_inc(xnT_copied, 1)

            def high(n, w):
                eng.wait_ge(rotated, 4 * n + 2 * w + 2)
                wait_past(eng, parts_out, 32 * n)
                eng.copy(parts[:, w, 0], rotated_in(n, w)).then_inc(hi_done, 1)

            def middle(n, w):
                eng.wait_ge(rem_done, 2 * n + w + 1)
                eng.copy(parts[:, w, 1], rotated_in(n, w)).then_inc(mid_done, 1)

            def parts_of_first(n):
                if n == 3:
                    for w in range(2):
                        high(0, w)
                        middle(0, w)
                    high(1, 0)

            each_batch(eng, normalise, parts_of_first)
            copy_turned(NB - 1, 1)
            middle(1, 0)
            high(1, 1)
            middle(1, 1)
            for parts_of, raw in zip(w_parts, (wq_sb, wk_sb)):
                eng.copy(parts_of[:, 0], raw).then_inc(w_high, 1)
            nw = NC * D
            eng.wait_ge(wquant, 7)
            eng.mul(qv[:, 0:nw], wf_sb[:, :, :].rearrange("p c n -> p (c n)"), scale[:, 1:2]).then_inc(wf_scaled, 1)
            eng.wait_ge(w_in, 16 * 4)
            eng.mul(wo_sb[:, :, :], wo_sb[:, :, :], scale[:, 0:1]).then_inc(wo_scaled, 1)
            eng.wait_ge(wo_scaled, 1)
            eng.mul(wo_sb[:, :, :], wo_sb[:, :, :], scale[:, 1:2]).then_inc(wo_scaled, 1)
            def iteration(b, par, stages, before):
                n = b + 2

                if 3 in stages and 3 not in before:
                    eng.wait_ge(consts, 7)
                    eng.wait_ge(amax_done, NB)
                    eng.wait_ge(w_split, 2)
                if 4 in stages and 4 not in before:
                    eng.wait_ge(wquant, 10)

                def split_x():
                    wait_past(eng, full["qk"], 4 * n)
                    eng.copy(x_parts[:, 0], xnT[:, :, bass.ds(n * T, T)]).then_inc(x_high, 1)

                def exp(s):
                    g, u = divmod(s, 5)
                    if g > 0 or not isinstance(b, int) or b > 0:
                        eng.wait_ge(pv_done, 12 * b + 3 * (g - 1) + (1, 1, 2, 2, 3)[u])
                    for half in range(2):
                        eng.wait_ge(st_full, 2 * (SLOTS * b + s) + half + 1)
                        eng.activation(prob[u][:, half * T:(half + 1) * T], st_ps[ST_BANK[2 * s + half]][:, :],
                                       ACT.Exp, scale=SCALE).then_inc(exp_done, 1)

                def copy_v(i):
                    bank = shared["v", i]
                    eng.wait_ge(full["v"], 2 * b + i + 1)
                    if i == 0:
                        wait_past(eng, pv_done, 12 * b)
                    eng.copy(v_sb[:, 2 * i:2 * i + 2, :, 0:DH],
                             bank[:, :].rearrange("p (k h w) -> p k h w", k=2, h=H)).then_inc(v_copied, 1)

                def copy_heads(bb, g):
                    eng.wait_ge(pv_done, 12 * bb + 3 * (g + 1))
                    if g == 0:
                        wait_past(eng, full["o"], 4 * bb)
                    eng.copy(heads[:, g, :], o_ps[:, :]).then_inc(heads_copied, 1)

                def copy_at(qb):
                    bank = shared["at", qb]
                    eng.wait_ge(full["at"], 4 * (b - 1) + qb + 1)
                    wait_past(eng, full["fin"], 4 * (b - 1) + max(qb - 1, 0))
                    eng.copy(attnT[:, qb % 2, :, :], bank[:, 0:D].rearrange("p (c n) -> p c n", c=NC))\
                       .then_inc(at_copied, 1)

                for s in range(SLOTS):
                    if 1 in stages and s == 0:
                        split_x()
                    if 3 in stages:
                        exp(s)
                    if 4 in stages and s == 0:
                        wait_past(eng, xq_done, b - 1)
                        eng.mul(qv[:, :].rearrange("p (c t) -> p c t", c=NC),
                                xnT[:, :, bass.ds((b - 1) * T, T)], scale[:, 0:1]).then_inc(qv_done, 1)
                    if 4 in stages and s == 2:
                        copy_heads(b - 1, NG - 1)
                    for slot, kind, k in work(stages):
                        if kind in ("v", "at") and s == slot + (kind == "v"):
                            {"v": copy_v, "at": copy_at}[kind](k)
                    if 3 in stages and s in (7, 12, 17):
                        copy_heads(b, s // 5 - 1)
                    if 1 in stages:
                        if s in (4, 10):
                            high(n, s // 10)
                        if s in (6, 12):
                            middle(n, s // 12)

            run(eng, iteration)

        @block.tensor
        def _(eng):
            eng.wait_ge(consts, 6)

            def turn_rows(n, p):
                eng.wait_ge(xn_done, NQ * (n + 1))
                wait_past(eng, xnT_copied, 2 * (n - 1))
                for c in range(NC):
                    for t in range(NQ):
                        mm = eng.transpose(turn_ps[p][c][:, t * P:(t + 1) * P],
                                           xn[p][:, t, c * P:(c + 1) * P], ident[:, :])
                    mm.then_inc(xn_turned, 1)

            def project_whole(n, k, bank):
                w = (wq_sb, wk_sb)[k // 2]
                for c in range(NC):
                    mm = eng.matmul(bank[:, :], w[:, c, k % 2, :], xnT[:, c, bass.ds(n * T, T)],
                                    start=(c == 0), stop=(c == NC - 1))
                return mm

            def project(n, k, bank):
                eng.wait_ge(x_split, n - 1)
                terms = [(wp, xp, c) for wp, xp in ((0, 0), (0, 1), (1, 0)) for c in range(NC)]
                for i, (wp, xp, c) in enumerate(terms):
                    mm = eng.matmul(bank[:, :], w_parts[k // 2][:, wp, c, k % 2, :], x_parts[:, xp, c, :],
                                    start=(i == 0), stop=(i == len(terms) - 1))
                return mm

            def project_first(n):
                if n in (1, 3):
                    for k in (range(0, 2), range(2, 8))[n // 2]:
                        if k == 0:
                            eng.wait_ge(w_qk_in, 16 * 4)
                            eng.wait_ge(xnT_copied, 2)
                        if k >= 4:
                            eng.wait_ge(xnT_copied, 4)
                            eng.wait_ge(roped, k - 4 + 1)
                        project_whole(k // 4, k % 4, first_ps[k % 4]).then_inc(full["qk"], 1)

            each_batch(eng, turn_rows, project_first)
            eng.wait_ge(roped, 8)

            def spread_maxima(s):
                if s == 2:
                    eng.wait_ge(amax_done, NB + 3)
                    eng.transpose(o_ps[0:2, 0:P], amax2[:, :], ident[:, :]).then_inc(amax_turned, 1)
                if s == 4:
                    eng.wait_ge(wquant, 2)
                    eng.matmul(o_ps[:, 0:2], ones2[:, :], amax_d[:, :], start=True, stop=True)\
                       .then_inc(amax_turned, 1)

            eng.wait_ge(xnT_copied, 2 * NB)

            def iteration(b, par, stages, before):
                n = b + 1

                def scores(s):
                    g, u = divmod(s, 5)
                    if u == 0 and g % 2 == 0:
                        eng.wait_ge(shift_in[g // 2], 16 * (b + 1))
                    for half in range(2):
                        i = 2 * s + half
                        wait_past(eng, exp_done, HALVES * b + ST_BEFORE[i] + 1)
                        for j, kb, col in unit_parts(u, half):
                            h = g * HG + j
                            mm = eng.matmul(st_ps[ST_BANK[i]][:, col:col + T - kb * P],
                                            k_st[0:ROWS + SHIFT, par, h, kb * P:(kb + 1) * P],
                                            q_st[0:ROWS + SHIFT, par, h, kb * P:T], start=True, stop=True)
                        mm.then_inc(st_full, 1)
                        if half == 0 and 2 in stages:
                            scores_for_max(2 * s)

                def scores_for_max(f):
                    pair, m = divmod(f, len(MAX_BANKS))
                    if f % (BANKS // NG) == 0:
                        g = f // (BANKS // NG)
                        eng.wait_ge(stack_in[g], 16 * 6 * (n + 1))
                    wait_past(eng, max_done, ITEMS * n + (ITEMS_UP_TO[f - 2] if f >= 2 else ITEMS_UP_TO[f - 2] - ITEMS))
                    for i, qb, col in MAX_BANKS[m]:
                        h = 2 * pair + i
                        mm = eng.matmul(s_ps[f % 2][:, col:col + (qb + 1) * P],
                                        q_st[0:ROWS, 1 - par, h, qb * P:(qb + 1) * P],
                                        k_st[0:ROWS, 1 - par, h, 0:(qb + 1) * P], start=True, stop=True)
                    mm.then_inc(s_full, 1)

                def project_v(i):
                    bank = shared["v", i]
                    if i == 0:
                        eng.wait_ge(xnv_in, 16 * (b + 1))
                    for t in range(2):
                        for c in range(NC):
                            mm = eng.matmul(bank[:, t * D:(t + 1) * D],
                                            xn_v[:, c, (2 * i + t) * P:(2 * i + t + 1) * P],
                                            wv_sb[:, c, :], start=(c == 0), stop=(c == NC - 1))
                    return mm

                def turn_heads(qb):
                    bank = shared["o", qb]
                    eng.wait_ge(heads_copied, 4 * b)
                    for g in range(NG):
                        mm = eng.transpose(bank[:, g * P:(g + 1) * P], heads[:, g, qb * P:(qb + 1) * P],
                                           ident[:, :])
                    return mm

                def turn_attn(qb):
                    bank = shared["at", qb]
                    eng.wait_ge(normed, 4 * (b - 1) + qb + 1)
                    for c in range(NC):
                        mm = eng.transpose(bank[:, c * P:(c + 1) * P], attn[:, qb, c * P:(c + 1) * P],
                                           ident[:, :])
                    return mm

                def outputs(qb):
                    bank = shared["fin", qb]
                    eng.wait_ge(at_copied, 4 * (b - 1) + qb + 1)
                    for c in range(NC):
                        eng.matmul(bank[:, 0:D], attnT[:, qb % 2, c, :], wo_sb[:, c, :],
                                   start=(c == 0), stop=False)
                    if qb == 0:
                        eng.wait_ge(xq_done, b)
                    for c in range(NC):
                        mm = eng.matmul(bank[:, 0:D], xq[:, c, qb * P:(qb + 1) * P], wf_q[:, c, :],
                                        start=False, stop=(c == NC - 1))
                    return mm

                def turn_max(i):
                    bank = shared["mt", i]
                    eng.wait_ge(max_done, ITEMS * (b + ahead["mt"][i]) + ITEMS // 2 * (i + 1))
                    return eng.transpose(bank[0:H * NQ // 2, 0:P],
                                         rowmax[:, H * NQ // 2 * i:H * NQ // 2 * (i + 1)], ident[:, :])

                def pv(bb, g, step):
                    for kb in ((0,), (1, 3), (2,))[step]:
                        if kb == 0:
                            wait_past(eng, heads_copied, 4 * bb + g)
                        if g == 0 and kb < 2:
                            eng.wait_ge(v_copied, 2 * bb + kb + 1)
                        eng.wait_ge(masked, SLOTS * bb + 5 * g + (2, 4, 5)[step])
                        for u in ((0, 1), (2, 3), (4,))[step]:
                            for i, k, col in [(i, k, T * half + col) for half in range(2)
                                              for i, k, col in unit_parts(u, half)]:
                                if k == kb:
                                    mm = eng.matmul(o_ps[32 * i:32 * i + VW, kb * P:T],
                                                    v_sb[:, kb, g * HG + i, :],
                                                    prob[u][:, col:col + T - kb * P],
                                                    start=(kb == 0), stop=(kb == 2),
                                                    skip_group_check=True)
                    mm.then_inc(pv_done, 1)

                todo = work(stages)
                done_before = work(before)

                def bank_free(at):
                    bank = SHARED_BANK[todo[at][1:]]
                    past = [(b, m) for m in todo[:at] if SHARED_BANK[m[1:]] == bank] or \
                           [(b - 1, m) for m in done_before if SHARED_BANK[m[1:]] == bank]
                    if past:
                        b_, (_, kind, k) = past[-1]
                        done, per = reader[kind]
                        eng.wait_ge(done, per * (b_ + ahead[kind][k]) + k + 1)

                if 3 in stages and 3 not in before:
                    eng.wait_ge(consts, 8)
                    eng.wait_ge(w_in, 16 * 4)
                    eng.wait_ge(wquant, 3)
                    eng.wait_ge(w_split, 2)
                if 4 in stages and 4 not in before:
                    eng.wait_ge(wquant, 10)
                    eng.wait_ge(wo_scaled, 2)

                do = {"qk": lambda k: project(b + 2, k, shared["qk", k]), "v": project_v, "o": turn_heads, "at": turn_attn, "fin": outputs,
                      "mt": turn_max}
                for s in range(SLOTS):
                    if 3 in stages:
                        scores(s)
                    elif 2 in stages:
                        scores_for_max(2 * s)
                    if 2 in stages:
                        scores_for_max(2 * s + 1)
                        if 3 not in stages:
                            spread_maxima(s)
                    for at, item in enumerate(todo):
                        if item[0] != s:
                            continue
                        bank_free(at)
                        do[item[1]](item[2]).then_inc(full[item[1]], 1)
                    if 4 in stages and s < 2:
                        pv(b - 1, NG - 1, s + 1)
                    if 3 in stages:
                        for lag, step in ((3, 0), (5, 1), (6, 2)):
                            if s >= lag and (s - lag) % 5 == 0 and (s - lag) // 5 < NG:
                                pv(b, (s - lag) // 5, step)

            run(eng, iteration)


def kernel(L0_attn_X, L0_attn_W_q, L0_attn_W_k, L0_attn_W_v, L0_attn_W_o, L0_ffn_weight, L0_ffn_bias):
    import concourse.bacc as bacc
    from concourse.bass_utils import run_bass_kernel_spmd

    def turned(w):
        return np.ascontiguousarray(np.asarray(w).T)

    def pairs(w):
        return np.ascontiguousarray(np.asarray(w).reshape(H, J, 2, D).transpose(3, 2, 1, 0).reshape(D, 2, J * H))

    theta = (np.float32(10000.0) ** (np.float32(-2.0) * np.arange(J, dtype=np.float32) / np.float32(DH)))
    angles = (np.arange(T, dtype=np.float32)[:, None] * theta.astype(np.float32)[None, :]).T
    cos = np.ascontiguousarray(np.repeat(np.cos(angles), H, axis=0).astype(np.float32))
    sin = np.ascontiguousarray(np.repeat(np.sin(angles), H, axis=0).astype(np.float32))

    arrays = {"x": np.ascontiguousarray(np.asarray(L0_attn_X)), "wq": pairs(L0_attn_W_q), "wk": pairs(L0_attn_W_k),
              "wv": turned(L0_attn_W_v), "wo": turned(L0_attn_W_o), "wf": turned(L0_ffn_weight),
              "bias": np.ascontiguousarray(np.asarray(L0_ffn_bias)), "cos": cos, "sin": sin}
    nc = bacc.Bacc("TRN2", target_bir_lowering=False, num_devices=1)
    args = [nc.dram_tensor(f"{k}_dram", a.shape, F32, kind="ExternalInput").ap() for k, a in arrays.items()]
    args.append(nc.dram_tensor("out_dram", (NB, T, D), F32, kind="ExternalOutput").ap())
    attention_ffn_block(nc, *args)
    r = run_bass_kernel_spmd(nc, [{f"{k}_dram": a for k, a in arrays.items()}], core_ids=[0])
    return r.results[0]["out_dram"]
```
